# Optimizing a Trainium2 kernel written in Bass

```python
import numpy as np
import jax
import jax.numpy as jnp

def _softmax(x, axis=-1):
    return jax.nn.softmax(x, axis=axis)

def _gelu(x):
    return jax.nn.gelu(x, approximate=True)

def _silu(x):
    return jax.nn.silu(x)

def _sigmoid(x):
    return jax.nn.sigmoid(x)

def _layernorm(x, axis=-1, eps=1e-05):
    m = jnp.mean(x, axis=axis, keepdims=True)
    v = jnp.var(x, axis=axis, keepdims=True)
    return (x - m) / jnp.sqrt(v + eps)

def _scatter_add(tgt, idx, src, axis=0):
    return tgt.at[idx].add(src)

def _segment_sum(src, seg, n):
    return jax.ops.segment_sum(src, seg, n)
kernel_name = 'mk_seq_postln_d1_jaxref_r4_9938ad'

def setup_inputs(seed: int=0):
    np.random.seed(seed)
    _w = jnp.asarray

    def _L0_attn_setup():
        import jax, jax.numpy as jnp
        import numpy as np
        DIM = 256
        HEADS = 16
        HEAD_DIM = DIM // HEADS
        SCALE = float(HEAD_DIM ** (-0.25))
        ROPE_BASE = 10000.0

        def apply_rope(x):
            B, N, H, D = x.shape
            half = D // 2
            inv_freq = 1.0 / ROPE_BASE ** (jnp.arange(half, dtype=jnp.float32) / half)
            freqs = jnp.arange(N, dtype=jnp.float32)[:, None] * inv_freq[None, :]
            cos = jnp.cos(freqs)[None, :, None, :].astype(x.dtype)
            sin = jnp.sin(freqs)[None, :, None, :].astype(x.dtype)
            x1, x2 = (x[..., :half], x[..., half:])
            return jnp.concatenate([x1 * cos - x2 * sin, x1 * sin + x2 * cos], axis=-1)
        key = jax.random.key(seed)
        k1, k2, k3 = jax.random.split(key, 3)
        x = jax.random.normal(k1, (4, 1024, DIM), dtype=jnp.float32)
        w_qkv = jax.random.normal(k2, (DIM, 3 * DIM), dtype=jnp.float32) * 0.02
        w_out = jax.random.normal(k3, (DIM, DIM), dtype=jnp.float32) * 0.02
        return {'x': x, 'w_qkv': w_qkv, 'w_out': w_out}
    _L0_attn_in = _L0_attn_setup()

    def _L0_ffn_setup():
        import jax, jax.numpy as jnp
        import numpy as np
        TOP_K = 32
        TEMPERATURE = 1.0
        PARAM_SCALE = 0.02

        def _compose_weight(logits, A, B):
            vals, idx = jax.lax.top_k(logits, TOP_K)
            w = jax.nn.softmax(vals / TEMPERATURE)
            A_sel = A[idx]
            B_sel = B[idx]
            return jnp.einsum('k,kir,kro->io', w, A_sel, B_sel)
        key = jax.random.key(seed)
        ks = jax.random.split(key, 7)
        B, S, D, F, P, R = (2, 256, 256, 1024, 64, 64)
        x = jax.random.normal(ks[0], (B, S, D), dtype=jnp.float32)
        fc1_A = jax.random.normal(ks[1], (P, D, R), dtype=jnp.float32) * PARAM_SCALE
        fc1_B = jax.random.normal(ks[2], (P, R, F), dtype=jnp.float32) * PARAM_SCALE
        fc2_A = jax.random.normal(ks[3], (P, F, R), dtype=jnp.float32) * PARAM_SCALE
        fc2_B = jax.random.normal(ks[4], (P, R, D), dtype=jnp.float32) * PARAM_SCALE
        fc1_logits = jax.random.normal(ks[5], (P,), dtype=jnp.float32)
        fc2_logits = jax.random.normal(ks[6], (P,), dtype=jnp.float32)
        return {'x': x, 'fc1_A': fc1_A, 'fc1_B': fc1_B, 'fc2_A': fc2_A, 'fc2_B': fc2_B, 'fc1_logits': fc1_logits, 'fc2_logits': fc2_logits}
    _L0_ffn_in = _L0_ffn_setup()
    _d = {'L0_attn_x': _L0_attn_in['x'], 'L0_attn_w_qkv': _L0_attn_in['w_qkv'], 'L0_attn_w_out': _L0_attn_in['w_out'], 'L0_ffn_fc1_A': _L0_ffn_in['fc1_A'], 'L0_ffn_fc1_B': _L0_ffn_in['fc1_B'], 'L0_ffn_fc2_A': _L0_ffn_in['fc2_A'], 'L0_ffn_fc2_B': _L0_ffn_in['fc2_B'], 'L0_ffn_fc1_logits': _L0_ffn_in['fc1_logits'], 'L0_ffn_fc2_logits': _L0_ffn_in['fc2_logits']}
    _x0 = _d['L0_attn_x']
    _d['L0_attn_x'] = jax.random.normal(jax.random.fold_in(jax.random.key(seed), 1), (8, 1024, 256), dtype=_x0.dtype)
    del _x0
    return _d

def reference(L0_attn_x, L0_attn_w_qkv, L0_attn_w_out, L0_ffn_fc1_A, L0_ffn_fc1_B, L0_ffn_fc2_A, L0_ffn_fc2_B, L0_ffn_fc1_logits, L0_ffn_fc2_logits):

    def _L0_attn_ref(x, w_qkv, w_out):
        import jax, jax.numpy as jnp
        import numpy as np
        DIM = 256
        HEADS = 16
        HEAD_DIM = DIM // HEADS
        SCALE = float(HEAD_DIM ** (-0.25))
        ROPE_BASE = 10000.0

        def apply_rope(x):
            B, N, H, D = x.shape
            half = D // 2
            inv_freq = 1.0 / ROPE_BASE ** (jnp.arange(half, dtype=jnp.float32) / half)
            freqs = jnp.arange(N, dtype=jnp.float32)[:, None] * inv_freq[None, :]
            cos = jnp.cos(freqs)[None, :, None, :].astype(x.dtype)
            sin = jnp.sin(freqs)[None, :, None, :].astype(x.dtype)
            x1, x2 = (x[..., :half], x[..., half:])
            return jnp.concatenate([x1 * cos - x2 * sin, x1 * sin + x2 * cos], axis=-1)
        B, N, D = x.shape
        qkv = x @ w_qkv
        q, k, v = jnp.split(qkv, 3, axis=-1)
        q = q.reshape(B, N, HEADS, HEAD_DIM)
        k = k.reshape(B, N, HEADS, HEAD_DIM)
        v = v.reshape(B, N, HEADS, HEAD_DIM)
        q = apply_rope(q)
        k = apply_rope(k)
        q = jax.nn.elu(q * SCALE) + 1.0
        k = jax.nn.elu(k * SCALE) + 1.0
        qT = jnp.moveaxis(q, 1, 0)
        kT = jnp.moveaxis(k, 1, 0)
        vT = jnp.moveaxis(v, 1, 0)
        kv0 = jnp.zeros((B, HEADS, HEAD_DIM, HEAD_DIM), dtype=q.dtype)
        ks0 = jnp.zeros((B, HEADS, HEAD_DIM), dtype=q.dtype)

        def step(carry, qkv_t):
            kv, ks = carry
            qt, kt, vt = qkv_t
            kv = kv + jnp.einsum('bhd,bhm->bhdm', kt, vt)
            ks = ks + kt
            denom = jnp.maximum(jnp.einsum('bhd,bhd->bh', qt, ks), 1e-06)
            out_t = jnp.einsum('bhd,bhdm->bhm', qt, kv) / denom[..., None]
            return ((kv, ks), out_t)
        _, outT = jax.lax.scan(step, (kv0, ks0), (qT, kT, vT))
        out = jnp.moveaxis(outT, 0, 1).reshape(B, N, D)
        return out @ w_out

    def _L0_ffn_ref(x, fc1_A, fc1_B, fc2_A, fc2_B, fc1_logits, fc2_logits):
        import jax, jax.numpy as jnp
        import numpy as np
        TOP_K = 32
        TEMPERATURE = 1.0
        PARAM_SCALE = 0.02

        def _compose_weight(logits, A, B):
            vals, idx = jax.lax.top_k(logits, TOP_K)
            w = jax.nn.softmax(vals / TEMPERATURE)
            A_sel = A[idx]
            B_sel = B[idx]
            return jnp.einsum('k,kir,kro->io', w, A_sel, B_sel)
        W1 = _compose_weight(fc1_logits, fc1_A, fc1_B)
        W2 = _compose_weight(fc2_logits, fc2_A, fc2_B)
        h = jax.nn.gelu(jnp.einsum('bsd,df->bsf', x, W1))
        return jnp.einsum('bsf,fd->bsd', h, W2)
    x = L0_attn_x
    x = _layernorm(x + _L0_attn_ref(x, L0_attn_w_qkv, L0_attn_w_out), axis=-1)
    x = _layernorm(x + _L0_ffn_ref(x, L0_ffn_fc1_A, L0_ffn_fc1_B, L0_ffn_fc2_A, L0_ffn_fc2_B, L0_ffn_fc1_logits, L0_ffn_fc2_logits), axis=-1)
    return x

_drawn_inputs = setup_inputs


def setup_inputs(seed=0):
    import zlib

    import numpy as np

    out = dict(_drawn_inputs(seed))
    spreads = {}
    factors = {'L0_attn_w_qkv': 6.397,
     'L0_attn_w_out': 6.432,
     'L0_ffn_fc1_A': 8.0,
     'L0_ffn_fc1_B': 8.0,
     'L0_ffn_fc2_A': 8.0,
     'L0_ffn_fc2_B': 8.0,
     'L0_ffn_fc1_logits': 8.0,
     'L0_ffn_fc2_logits': 8.0}
    for name, (base, spread) in spreads.items():
        noise = np.random.default_rng([zlib.crc32(name.encode()), seed]).standard_normal(out[name].shape)
        drawn = base * np.exp(spread * noise) if base else spread * noise
        out[name] = jnp.asarray(drawn.astype(out[name].dtype))
    for name, factor in factors.items():
        out[name] = (out[name] * factor).astype(out[name].dtype)
    return out
```

```python
from contextlib import ExitStack

import concourse.bass as bass
from concourse import mybir

F32 = mybir.dt.float32
U32 = mybir.dt.uint32
ALU = mybir.AluOpType
ACT = mybir.ActivationFunctionType
AX = mybir.AxisListType

P = 128
BATCH, SEQ, DIM = 8, 1024, 256
HEADS, HD = 16, 16
HALF = 64
TILES = BATCH * SEQ // P
TILES_PER_SEQ = SEQ // P
KT = DIM // P
FFN = 1024
PRIMS, TOPK, RANK = 64, 32, 64
PAIRS = TOPK // 2
SLOTS = 4
ROUNDS = PAIRS // SLOTS
GROUP = 4
GROUPS = TILES // GROUP
FB = FFN // P
RING = 4
LN_EPS = 1e-5
DEN_MIN = 1e-6
NEG = -3.0e38
CONSTS = dict(tri=P, tri_rest=P, score_mask=HALF, head_mask=P, ident=P, even=1, odd=1)


def const_columns():
    at, out = 0, {}
    for name, n in CONSTS.items():
        out[name] = (at, at + n)
        at += n
    return out, at


def build_program(nc, xin, x, w_qkv, w_out, consts, selectors, logits, factors, out):
    with ExitStack() as ctx:
        def sb(name, shape, dt=F32):
            return ctx.enter_context(nc.sbuf_tensor(name, shape, dt))

        def sem(name):
            return ctx.enter_context(nc.semaphore(name))

        psum = ctx.enter_context(nc.psum_tensor("psum", [P, 8, 512], F32))
        bank = [psum[:, i, :] for i in range(8)]

        stream = sb("stream", [P, TILES, DIM])
        cols, ncols = const_columns()
        const_sb = sb("const_sb", [P, ncols])

        def const(name):
            return const_sb[:, cols[name][0]:cols[name][1]]

        sel_sb = sb("sel_sb", [2, 4, P])
        wqkv_sb = sb("wqkv_sb", [P, KT, 3 * DIM])
        wout_sb = sb("wout_sb", [P, KT, DIM])
        logit_sb = sb("logit_sb", [2, PRIMS])
        top_val = sb("top_val", [2, TOPK])
        top_idx = sb("top_idx", [2, TOPK], U32)
        neg_max = sb("neg_max", [2, 1])
        top_exp = sb("top_exp", [2, TOPK])
        top_sum = sb("top_sum", [2, 1])
        top_inv = sb("top_inv", [2, 1])
        top_w = sb("top_w", [2, TOPK])
        factor_w = sb("factor_w", [P, 2, PAIRS])
        xin_sb = sb("xin_sb", [P, 2, DIM + 2 * HD])
        rope_cos = sb("rope_cos", [P, 2 * DIM])
        rope_sin = sb("rope_sin", [P, 2 * DIM])
        roped = sb("roped", [P, 2 * DIM])
        feat_exp = sb("feat_exp", [P, 2 * DIM])
        feat_relu = sb("feat_relu", [P, 2 * DIM])
        feat = sb("feat", [P, 2, 2 * DIM])
        v_pad = sb("v_pad", [P, 2, HEADS, 2 * HD])
        den_prod = sb("den_prod", [P, DIM])
        den = sb("den", [P, HEADS])
        den_max = sb("den_max", [P, HEADS])
        den_inv = sb("den_inv", [P, HEADS])
        q_norm = sb("q_norm", [P, DIM])
        qT = sb("qT", [P, KT, P])
        kT = sb("kT", [P, 2, KT, P])
        state_sb = sb("state_sb", [P, 2, KT, P])
        scores_sb = sb("scores_sb", [P, 4, 4, HALF])
        oT = sb("oT", [P, KT, P])
        fence_out = sb("fence_out", [P, 1])
        stats1 = sb("stats1", [P, TILES, 6])
        mean1 = sb("mean1", [P, TILES])
        moment_sum = sb("moment_sum", [P, TILES])
        moment_dif = sb("moment_dif", [P, TILES])
        moment_m2 = sb("moment_m2", [P, TILES])
        moment_var = sb("moment_var", [P, TILES])
        moment_sq = sb("moment_sq", [P, TILES])
        var1 = sb("var1", [P, TILES])
        exponent = sb("exponent", [P, TILES])
        rstd1 = sb("rstd1", [P, TILES])
        slot = sb("slot", [P, SLOTS, DIM + FFN])
        w1_sb = sb("w1_sb", [P, KT, FFN])
        w2_sb = sb("w2_sb", [P, FB, DIM])
        x1_group = sb("x1_group", [P, GROUP, DIM])
        x1T = sb("x1T", [P, KT, GROUP * P])
        hT = sb("hT", [P, FB, GROUP * P])
        stats2 = sb("stats2", [P, GROUP, 6])
        mean2 = sb("mean2", [P, GROUP])
        var2 = sb("var2", [P, GROUP])
        rstd2 = sb("rstd2", [P, GROUP])

        b_qk, b_vy, b_acc, b_o = bank[0:4]
        b_ksum, b_state = b_acc[:, 0:DIM], b_acc[:, DIM:2 * DIM]
        b_scores = psum[:, 4:8, :]
        b_tr = bank[7]

        s_logits, s_const, s_sel, s_wqkv, s_wout = (sem(n) for n in (
            "logits_loaded", "const_loaded", "sel_loaded", "wqkv_loaded", "wout_loaded"))
        s_stream = [sem(f"stream_loaded{b}") for b in range(BATCH)]
        s_xin = [sem("xin_loaded0"), sem("xin_loaded1")]
        topk_step, topk_done, top_exp_done, top_w_done, bcast_ready, factor_w_ready, zeroed = (
            sem(n) for n in ("topk_step", "topk_done", "top_exp_done", "top_w_done", "bcast_ready",
                             "factor_w_ready", "zeroed"))
        (qk_ready, v_ready, qk_used, v_used, roped_ready, exp_done, relu_done, feat_ready, carry_ready,
         ksum_ready, ksum_used, den_prod_done, den_done, den_max_done, den_inv_done, qnorm_ready, state_ready, mid_ready, acc_done,
                  own_done, tr_ready, qkT_ready, ko_ready, scores_ready, scores_masked, o_ready, oT_ready, y_ready, y_used,
         stats1_ready) = (sem(n) for n in (
             "qk_ready", "v_ready", "qk_used", "v_used", "roped_ready", "exp_done", "relu_done",
             "feat_ready", "carry_ready", "ksum_ready", "ksum_used", "den_prod_done", "den_done",
             "den_max_done", "den_inv_done", "qnorm_ready", "state_ready", "mid_ready", "acc_done", "own_done", "tr_ready",
             "qkT_ready", "ko_ready", "scores_ready", "scores_masked", "o_ready", "oT_ready", "y_ready",
             "y_used", "stats1_ready"))
        s_slot = [sem(f"slot_loaded{s}") for s in range(SLOTS)]
        (slot_scaled, slot_used, banks_zeroed, moment_step, w1_act, w1_dve, w2_act, w2_dve, var1_ready,
         rstd1_ready) = (sem(n) for n in (
             "slot_scaled", "slot_used", "banks_zeroed", "moment_step", "w1_act", "w1_dve",
             "w2_act", "w2_dve", "var1_ready", "rstd1_ready"))
        (x1_ready, x1_copied, x1T_psum, x1T_act, x1T_dve, h_psum, h_act, y2_psum, y2_added, stats2_ready,
         var2_ready, rstd2_ready, result_ready, stored) = (sem(n) for n in (
             "x1_ready", "x1_copied", "x1T_psum", "x1T_act", "x1T_dve", "h_psum", "h_act", "y2_psum", "y2_added",
             "stats2_ready", "var2_ready", "rstd2_ready", "result_ready", "stored"))

        block = ctx.enter_context(nc.Block())

        def tile_loop(engine, step):
            step(0, False, True, 0, 1)
            with engine.Fori(1, TILES // 2) as i:
                step(2 * i - 1, True, True, 1, i + 1)
                step(2 * i, True, True, 0, i + 1)
            step(TILES - 1, True, False, 1, None)

        @block.sync
        def _(sp):
            sp.dma_start(logit_sb[:], logits).then_inc(s_logits, 16)
            for p in range(2):
                sp.dma_start(xin_sb[:, p, :], xin[p]).then_inc(s_xin[p], 16)
            sp.dma_start(wqkv_sb[:], w_qkv.rearrange("(k p) n -> p k n", p=P)).then_inc(s_wqkv, 16)
            sp.dma_start(const_sb[:], consts).then_inc(s_const, 16)
            sp.dma_start(sel_sb[:], selectors).then_inc(s_sel, 16)
            sp.dma_start(wout_sb[:], w_out.rearrange("(k p) n -> p k n", p=P)).then_inc(s_wout, 16)
            stream_in = x.rearrange("(b t p) d -> b p t d", b=BATCH, p=P)
            for b in range(BATCH):
                at = b * TILES_PER_SEQ
                sp.dma_start(stream[:, at:at + TILES_PER_SEQ, :], stream_in[b]).then_inc(s_stream[b], 16)

            def gather(fc, n, s, first):
                if not first:
                    sp.wait_ge(slot_used, fc * PAIRS + n - SLOTS + 1)
                for half in range(2):
                    k = sp.value_load(top_idx[fc:fc + 1, bass.ds(2 * n + half, 1)], min_val=0, max_val=PRIMS - 1)
                    sp.dma_start(slot[half * RANK:(half + 1) * RANK, s, :],
                                 factors[fc][bass.ds(k, 1)].rearrange("a r c -> (a r) c")).then_inc(s_slot[s], 16)

            sp.wait_ge(topk_done, 1)
            for s in range(SLOTS):
                gather(0, s, s, True)

            def load_tile(t, p):
                sp.wait_ge(v_ready, t - 1)
                sp.wait_ge(qk_used, t - 1)
                sp.dma_start(xin_sb[:, p, :], xin[bass.ds(t, 1)].rearrange("a p c -> (a p) c")).then_inc(s_xin[p], 16)

            with sp.Fori(1, TILES // 2) as i:
                load_tile(2 * i, 0)
                load_tile(2 * i + 1, 1)
            with sp.Fori(1, ROUNDS) as r:
                for s in range(SLOTS):
                    gather(0, r * SLOTS + s, s, False)
            with sp.Fori(0, ROUNDS) as r:
                for s in range(SLOTS):
                    gather(1, r * SLOTS + s, s, False)
            result_out = out.rearrange("(g t p) d -> g p t d", t=GROUP, p=P)
            with sp.Fori(0, GROUPS) as g:
                sp.wait_ge(result_ready, g + 1)
                sp.dma_start(result_out[bass.ds(g, 1)].rearrange("a p t d -> p (a t) d"),
                             stream[:, bass.ds(g * GROUP, GROUP), :]).then_inc(stored, 16)
            sp.wait_ge(stored, 16 * GROUPS)

        @block.gpsimd
        def _(pool):
            def rope_sum(n):
                pool.wait_ge(qk_used, n + 1)
                if not (isinstance(n, int) and n == 0):
                    pool.wait_ge(exp_done, n)
                    pool.wait_ge(relu_done, n)
                nc.gpsimd.tensor_tensor(roped[:], rope_cos[:], rope_sin[:], ALU.add).then_inc(roped_ready, 1)

            def step(t, has_prev, has_next, parity, loads):
                if has_next:
                    rope_sum(t + 1)

            nc.gpsimd.memset(exponent[:], -0.5).then_inc(zeroed, 1)
            rope_sum(0)
            tile_loop(pool, step)
            pool.wait_ge(var1_ready, 1)
            pool.wait_ge(zeroed, 2)
            nc.gpsimd.tensor_tensor(rstd1[:], var1[:], exponent[:], ALU.pow).then_inc(rstd1_ready, 1)

            def copy_x1(g):
                pool.wait_ge(x1_ready, (g + 1) * GROUP)
                if not (isinstance(g, int) and g == 0):
                    pool.wait_ge(x1T_psum, 2 * g)
                nc.gpsimd.tensor_copy(x1_group[:], stream[:, bass.ds(g * GROUP, GROUP), :]).then_inc(x1_copied, 1)

            def group_step(g, has_next):
                if has_next:
                    copy_x1(g + 1)
                pool.wait_ge(var2_ready, g + 1)
                nc.gpsimd.tensor_tensor(rstd2[:], var2[:], exponent[:, 0:GROUP], ALU.pow).then_inc(rstd2_ready, 1)

            copy_x1(0)
            with pool.Fori(0, GROUPS - 1) as g:
                group_step(g, True)
            group_step(GROUPS - 1, False)

        @block.scalar
        def _(act):
            act.wait_ge(topk_done, 1)
            nc.scalar.activation(top_exp[:], top_val[:], ACT.Exp, bias=neg_max[:, 0:1],
                                 accum_out=top_sum[:]).then_inc(top_exp_done, 1)

            def move_v(n, p, t):
                act.wait_ge(v_ready, n + 1)
                if t is None:
                    act.wait_ge(zeroed, 2)
                elif not (isinstance(t, int) and t == 0):
                    act.wait_ge(o_ready, t)
                dst = v_pad[:, p].rearrange("k (a b) c -> k a (b c)", b=2)
                dst = dst.rearrange("k a (b c) -> k a b c", c=HD)[:, :, 0:4:3, :]
                nc.scalar.activation(dst, b_vy[:, 0:DIM].rearrange("k (a b c) -> k a b c", b=2, c=HD),
                                     ACT.Copy).then_inc(v_used, 1)

            def features(n):
                act.wait_ge(roped_ready, n + 1)
                if not (isinstance(n, int) and n == 0):
                    act.wait_ge(feat_ready, n)
                nc.scalar.activation(feat_exp[:], roped[:], ACT.Exp).then_inc(exp_done, 1)
                nc.scalar.activation(feat_relu[:], roped[:], ACT.Relu).then_inc(relu_done, 1)

            def step(t, has_prev, has_next, parity, loads):
                if has_next:
                    move_v(t + 1, 1 - parity, t)
                act.wait_ge(tr_ready, t + 1)
                if has_prev:
                    act.wait_ge(o_ready, t)
                nc.scalar.activation(qT[:], b_tr[:, 0:DIM].rearrange("p (k n) -> p k n", k=KT),
                                     ACT.Copy).then_inc(qkT_ready, 1)
                nc.scalar.activation(kT[:, 0], b_tr[:, DIM:2 * DIM].rearrange("p (k n) -> p k n", k=KT),
                                     ACT.Copy, scale=const("even")).then_inc(qkT_ready, 1)
                if has_next:
                    features(t + 1)
                act.wait_ge(o_ready, t + 1)
                if has_prev:
                    act.wait_ge(y_ready, t)
                nc.scalar.activation(oT[:], b_o[:, 0:DIM].rearrange("p (k n) -> p k n", k=KT),
                                     ACT.Copy).then_inc(oT_ready, 1)

            act.wait_ge(s_const, 16)
            move_v(0, 0, None)
            features(0)
            tile_loop(act, step)

            act.wait_ge(slot_used, PAIRS)
            for n in range(2):
                nc.scalar.activation(w1_sb[:, 0, n * 512:(n + 1) * 512], bank[n], ACT.Copy).then_inc(w1_act, 1)
            act.wait_ge(slot_used, 2 * PAIRS)
            for f in range(2):
                nc.scalar.activation(w2_sb[:, 2 * f:2 * f + 2, :], bank[4 + f].rearrange("p (f n) -> p f n", f=2),
                                     ACT.Copy).then_inc(w2_act, 1)

            def move_x1T(g):
                act.wait_ge(x1T_psum, 2 * g + 1)
                nc.scalar.activation(x1T[:, 0, :], bank[4], ACT.Copy).then_inc(x1T_act, 1)

            def group_step(g, has_next):
                for f in range(FB):
                    act.wait_ge(h_psum, g * FB + f + 1)
                    if f == 0 and not (isinstance(g, int) and g == 0):
                        act.wait_ge(y2_psum, g * GROUP)
                    nc.scalar.activation(hT[:, f, :], bank[f % RING], ACT.Gelu_apprx_tanh).then_inc(h_act, 1)
                if has_next:
                    move_x1T(g + 1)

            move_x1T(0)
            group_step(0, True)
            with act.Fori(1, GROUPS - 1) as g:
                group_step(g, True)
            group_step(GROUPS - 1, False)

        @block.vector
        def _(dve):
            steps = [0]

            def chained(instruction):
                steps[0] += 1
                instruction.then_inc(topk_step, 1)
                dve.wait_ge(topk_step, steps[0])

            dve.wait_ge(s_logits, 16)
            for r in range(TOPK // 8):
                at = slice(8 * r, 8 * r + 8)
                chained(nc.vector.max(top_val[:, at], logit_sb[:]))
                chained(nc.vector.max_index(top_idx[:, at], top_val[:, at], logit_sb[:]))
                if r < TOPK // 8 - 1:
                    chained(nc.vector.match_replace(logit_sb[:], top_val[:, at], logit_sb[:], NEG))
            nc.vector.tensor_scalar(neg_max[:], top_val[:, 0:1], -1.0, None, ALU.mult).then_inc(topk_done, 1)
            nc.vector.memset(v_pad[:], 0.0).then_inc(zeroed, 1)
            dve.wait_ge(top_exp_done, 1)
            chained(nc.vector.reciprocal(top_inv[:], top_sum[:]))
            nc.vector.tensor_scalar(top_w[:], top_exp[:], top_inv[:, 0:1], None, ALU.mult).then_inc(top_w_done, 1)
            dve.wait_ge(bcast_ready, 1)
            nc.vector.tensor_copy(factor_w[:], b_o[:, 0:2 * PAIRS].rearrange("p (f n) -> p f n", f=2))\
                .then_inc(factor_w_ready, 1)
            dve.wait_ge(s_const, 16)

            def rope(n, p):
                dve.wait_ge(qk_ready, n + 1)
                if not (isinstance(n, int) and n == 0):
                    dve.wait_ge(roped_ready, n)
                qk = b_qk.rearrange("p (h c) -> p h c", c=HD)
                cos = xin_sb[:, p, DIM:DIM + HD].unsqueeze(1).broadcast_to([P, 2 * HEADS, HD])
                nc.vector.tensor_tensor(rope_cos[:].rearrange("p (h c) -> p h c", c=HD), qk, cos, ALU.mult)
                sin = xin_sb[:, p, DIM + HD:DIM + 2 * HD]
                half = HD // 2
                nc.vector.tensor_tensor(
                    rope_sin[:].rearrange("p (h c) -> p h c", c=HD)[:, :, 0:half], qk[:, :, half:HD],
                    sin[:, 0:half].unsqueeze(1).broadcast_to([P, 2 * HEADS, half]), ALU.mult)
                nc.vector.tensor_tensor(
                    rope_sin[:].rearrange("p (h c) -> p h c", c=HD)[:, :, half:HD], qk[:, :, 0:half],
                    sin[:, half:HD].unsqueeze(1).broadcast_to([P, 2 * HEADS, half]), ALU.mult).then_inc(qk_used, 1)

            def finish_features(n, p):
                dve.wait_ge(exp_done, n + 1)
                dve.wait_ge(relu_done, n + 1)
                nc.vector.scalar_tensor_tensor(out=feat[:, p, :], in0=feat_exp[:], scalar=1.0, in1=feat_relu[:],
                                               op0=ALU.min, op1=ALU.add).then_inc(feat_ready, 1)

            def mask_state(which):
                return nc.vector.tensor_tensor(
                    state_sb[:, which], b_state[:, 0:DIM].rearrange("p (k n) -> p k n", k=KT),
                    const("head_mask").unsqueeze(1).broadcast_to([P, KT, P]), ALU.mult)

            def carry(t, has_prev, new_sequence):
                if has_prev:
                    dve.wait_ge(state_ready, 2 * t)
                    dve.wait_ge(acc_done, t)
                    dve.wait_ge(o_ready, t)
                if new_sequence is True:
                    nc.vector.memset(b_acc, 0.0).then_inc(topk_step, 1)
                    dve.wait_ge(topk_step, steps[0] + 1)
                elif new_sequence is not None:
                    with dve.If_eq(dve.to_reg(new_sequence % (TILES_PER_SEQ // 2)), 0):
                        nc.vector.memset(b_acc, 0.0)
                        nc.vector.drain()
                mask_state(0).then_inc(carry_ready, 1)

            def fence(semaphore, value):
                dve.wait_ge(semaphore, value)
                nc.vector.tensor_copy(fence_out[:], const("even"))

            def moments(stats, n, base, mean, var, signal):
                v = nc.vector
                v.tensor_tensor(moment_sum[:, 0:n], stats[:, :, 1], stats[:, :, 4], ALU.add)
                v.tensor_tensor(moment_dif[:, 0:n], stats[:, :, 1], stats[:, :, 4], ALU.subtract)
                v.tensor_tensor(moment_m2[:, 0:n], stats[:, :, 2], stats[:, :, 5], ALU.add).then_inc(moment_step, 1)
                dve.wait_ge(moment_step, base + 1)
                v.tensor_scalar(mean[:], moment_sum[:, 0:n], 0.5, None, ALU.mult)
                v.tensor_tensor(moment_sq[:, 0:n], moment_dif[:, 0:n], moment_dif[:, 0:n], ALU.mult)
                v.tensor_scalar(moment_var[:, 0:n], moment_m2[:, 0:n], 1.0 / DIM, LN_EPS, ALU.mult, ALU.add)\
                    .then_inc(moment_step, 1)
                dve.wait_ge(moment_step, base + 2)
                v.scalar_tensor_tensor(out=var[:], in0=moment_sq[:, 0:n], scalar=0.25, in1=moment_var[:, 0:n],
                                       op0=ALU.mult, op1=ALU.add).then_inc(signal, 1)

            def layer_norm1(n):
                dve.wait_ge(y_ready, n + 1)
                row = stream[:, bass.ds(n, 1), :].rearrange("p a d -> p (a d)")
                nc.vector.tensor_tensor(row, b_vy[:, DIM:2 * DIM], row, ALU.add).then_inc(y_used, 1)
                fence(y_used, n + 1)
                nc.vector.bn_stats(stats1[:, bass.ds(n, 1), :].rearrange("p a d -> p (a d)"), row).then_inc(stats1_ready, 1)

            def step(t, has_prev, has_next, parity, loads):
                if isinstance(t, int):
                    carry(t, has_prev, True if t == 0 else None)
                else:
                    carry(t, has_prev, loads - 1 if parity == 0 else None)
                if has_next:
                    rope(t + 1, 1 - parity)
                dve.wait_ge(ksum_ready, t + 1)
                nc.vector.tensor_tensor(den_prod[:], feat[:, parity, 0:DIM], b_ksum[:, 0:DIM], ALU.mult).then_inc(ksum_used, 1)
                dve.wait_ge(ksum_used, t + 1)
                nc.vector.tensor_reduce(den[:], den_prod[:].rearrange("p (h c) -> p h c", c=HD), AX.X, ALU.add)\
                    .then_inc(den_done, 1)
                dve.wait_ge(den_done, t + 1)
                nc.vector.tensor_scalar(den_max[:], den[:], DEN_MIN, None, ALU.max).then_inc(den_max_done, 1)
                dve.wait_ge(den_max_done, t + 1)
                nc.vector.reciprocal(den_inv[:], den_max[:]).then_inc(den_inv_done, 1)
                dve.wait_ge(den_inv_done, t + 1)
                nc.vector.tensor_tensor(q_norm[:].rearrange("p (h c) -> p h c", c=HD),
                                        feat[:, parity, 0:DIM].rearrange("p (h c) -> p h c", c=HD),
                                        den_inv[:].unsqueeze(2).broadcast_to([P, HEADS, HD]), ALU.mult).then_inc(qnorm_ready, 1)
                dve.wait_ge(state_ready, 2 * t + 1)
                mask_state(1).then_inc(mid_ready, 1)
                if has_prev:
                    layer_norm1(t - 1)
                dve.wait_ge(tr_ready, t + 1)
                dve.wait_ge(qkT_ready, 2 * t + 2)
                nc.vector.tensor_scalar(kT[:, 1], b_tr[:, DIM:2 * DIM].rearrange("p (k n) -> p k n", k=KT),
                                        const("odd"), None, ALU.mult).then_inc(ko_ready, 1)
                for part in range(2):
                    dve.wait_ge(scores_ready, 2 * t + part + 1)
                    tiles = slice(2 * part, 2 * part + 2)
                    nc.vector.tensor_tensor(
                        scores_sb[:, tiles], b_scores[:, tiles, 0:4 * HALF].rearrange("p r (h q) -> p r h q", h=4),
                        const("score_mask").unsqueeze(1).unsqueeze(1).broadcast_to([P, 2, 4, HALF]),
                        ALU.mult).then_inc(scores_masked, 1)
                if has_next:
                    finish_features(t + 1, 1 - parity)

            for b in range(BATCH):
                dve.wait_ge(s_stream[b], 16)
            rope(0, 0)
            finish_features(0, 0)
            tile_loop(dve, step)
            layer_norm1(TILES - 1)
            dve.wait_ge(stats1_ready, TILES)
            moments(stats1, TILES, 0, mean1, var1, var1_ready)

            dve.wait_ge(oT_ready, TILES)
            for b in bank:
                last = nc.vector.memset(b, 0.0)
            last.then_inc(banks_zeroed, 1)
            dve.wait_ge(factor_w_ready, 1)

            def scale_slot(fc, n, s):
                dve.wait_ge(s_slot[s], 32 * (fc * ROUNDS + n + 1))
                part = slot[:, s, 0:DIM]
                w = factor_w[:, fc, bass.ds(n * SLOTS + s, 1)]
                nc.vector.tensor_scalar(part, part, w, None, ALU.mult).then_inc(slot_scaled, 1)

            for fc in range(2):
                with dve.Fori(0, ROUNDS) as n:
                    for s in range(SLOTS):
                        scale_slot(fc, n, s)
                if fc == 0:
                    dve.wait_ge(slot_used, PAIRS)
                    for n in range(2):
                        nc.vector.tensor_copy(w1_sb[:, 1, n * 512:(n + 1) * 512], bank[2 + n]).then_inc(w1_dve, 1)
            dve.wait_ge(slot_used, 2 * PAIRS)
            for f in range(2, 4):
                nc.vector.tensor_copy(w2_sb[:, 2 * f:2 * f + 2, :], bank[4 + f].rearrange("p (f n) -> p f n", f=2))\
                    .then_inc(w2_dve, 1)

            dve.wait_ge(rstd1_ready, 1)

            def normalise1(g):
                for j in range(GROUP):
                    t = g * GROUP + j
                    row = stream[:, bass.ds(t, 1), :].rearrange("p a d -> p (a d)")
                    nc.vector.tensor_scalar(row, row, mean1[:, bass.ds(t, 1)],
                                            rstd1[:, bass.ds(t, 1)], ALU.subtract, ALU.mult).then_inc(x1_ready, 1)

            def move_x1T(g):
                dve.wait_ge(x1T_psum, 2 * g + 2)
                nc.vector.tensor_copy(x1T[:, 1, :], bank[5]).then_inc(x1T_dve, 1)

            def group_step(g, has_next):
                if has_next:
                    normalise1(g + 1)
                    move_x1T(g + 1)
                for j in range(GROUP):
                    n = g * GROUP + j
                    row = stream[:, bass.ds(n, 1), :].rearrange("p a d -> p (a d)")
                    dve.wait_ge(y2_psum, n + 1)
                    dve.wait_ge(x1_ready, n + 1)
                    nc.vector.tensor_tensor(row, bank[6 + j % 2][:, 0:DIM], row, ALU.add).then_inc(y2_added, 1)
                    fence(y2_added, n + 1)
                    nc.vector.bn_stats(stats2[:, j, :], row).then_inc(stats2_ready, 1)
                dve.wait_ge(stats2_ready, (g + 1) * GROUP)
                moments(stats2, GROUP, 2 + 2 * g, mean2, var2, var2_ready)
                dve.wait_ge(rstd2_ready, g + 1)
                for j in range(GROUP):
                    row = stream[:, bass.ds(g * GROUP + j, 1), :].rearrange("p a d -> p (a d)")
                    last = nc.vector.tensor_scalar(row, row, mean2[:, j:j + 1], rstd2[:, j:j + 1], ALU.subtract, ALU.mult)
                last.then_inc(result_ready, 1)

            normalise1(0)
            move_x1T(0)
            with dve.Fori(0, GROUPS - 1) as g:
                group_step(g, True)
            group_step(GROUPS - 1, False)

        @block.tensor
        def _(pe):
            mm = nc.tensor.matmul
            pe.wait_ge(s_sel, 16)
            pe.wait_ge(top_w_done, 1)
            for fc in range(2):
                for half in range(2):
                    last = mm(b_o[:, fc * PAIRS:(fc + 1) * PAIRS], sel_sb[:, 2 * fc + half, :], top_w[:, half:TOPK:2],
                              start=(half == 0), stop=(half == 1))
            last.then_inc(bcast_ready, 1)
            pe.wait_ge(s_wqkv, 16)
            pe.wait_ge(s_const, 16)

            def project(n, p, loads, t):
                pe.wait_ge(s_xin[p], 16 * loads)
                if t is not None:
                    pe.wait_ge(qk_used, t + 1)
                    pe.wait_ge(v_used, t + 1)
                    if not (isinstance(t, int) and t <= 1):
                        pe.wait_ge(y_used, t - 1)
                for k in range(KT):
                    last = mm(b_qk, xin_sb[:, p, k * P:(k + 1) * P], wqkv_sb[:, k, 0:2 * DIM],
                              start=(k == 0), stop=(k == KT - 1))
                last.then_inc(qk_ready, 1)
                for k in range(KT):
                    last = mm(b_vy[:, 0:DIM], xin_sb[:, p, k * P:(k + 1) * P], wqkv_sb[:, k, 2 * DIM:3 * DIM],
                              start=(k == 0), stop=(k == KT - 1))
                last.then_inc(v_ready, 1)

            def output_projection(t, v_count):
                pe.wait_ge(oT_ready, t + 1)
                pe.wait_ge(v_used, v_count)
                for k in range(KT):
                    last = mm(b_vy[:, DIM:2 * DIM], oT[:, k, :], wout_sb[:, k, :], start=(k == 0), stop=(k == KT - 1))
                last.then_inc(y_ready, 1)

            def add_to_state(half, parity, before_last=None):
                rows = slice(half * HALF, (half + 1) * HALF)
                values = v_pad[rows, parity].rearrange("k (a b) c -> k a (b c)", b=2)
                values = values.rearrange("k a (b c) -> k a b c", c=HD)[:, :, 0:4:3, :]
                for k in range(KT):
                    if k == KT - 1 and before_last is not None:
                        before_last()
                    last = mm(b_state[:, k * P:(k + 1) * P], feat[rows, parity, DIM + k * P:DIM + (k + 1) * P],
                              values[:, 4 * k:4 * k + 4], start=False, stop=True, skip_group_check=True)
                last.then_inc(state_ready, 1)

            def step(t, has_prev, has_next, parity, loads):
                if has_next:
                    project(t + 1, 1 - parity, loads, t)
                pe.wait_ge(feat_ready, t + 1)
                pe.wait_ge(carry_ready, t + 1)
                mm(b_ksum[:, 0:DIM], const("tri"), feat[:, parity, DIM:2 * DIM], start=False, stop=True,
                   skip_group_check=True).then_inc(ksum_ready, 1)
                if has_prev:
                    output_projection(t - 1, t + 2 if has_next else t + 1)
                pe.wait_ge(ksum_used, t + 1)
                pe.wait_ge(v_used, t + 1)
                add_to_state(0, parity)
                pe.wait_ge(qnorm_ready, t + 1)
                for k in range(KT):
                    nc.tensor.transpose(b_tr[:, k * P:(k + 1) * P], q_norm[:, k * P:(k + 1) * P], const("ident"))
                for k in range(KT):
                    last = nc.tensor.transpose(b_tr[:, DIM + k * P:DIM + (k + 1) * P],
                                               feat[:, parity, DIM + k * P:DIM + (k + 1) * P], const("ident"))
                last.then_inc(tr_ready, 1)
                pe.wait_ge(mid_ready, t + 1)
                mm(b_ksum[:, 0:DIM], const("tri_rest"), feat[:, parity, DIM:2 * DIM], start=False, stop=True,
                   skip_group_check=True).then_inc(acc_done, 1)
                pe.wait_ge(qkT_ready, 2 * t + 2)
                pe.wait_ge(ko_ready, t + 1)
                for part in range(2):
                    for h in range(4):
                        for half in range(2):
                            span = slice(half * HALF, (half + 1) * HALF)
                            for r in (2 * part, 2 * part + 1):
                                rows = slice(32 * r, 32 * r + 32)
                                last = mm(b_scores[span, r, h * HALF:(h + 1) * HALF],
                                          kT[rows, h % 2, h // 2, span], qT[rows, h // 2, span], start=True, stop=True)
                    last.then_inc(scores_ready, 1)
                if has_prev:
                    pe.wait_ge(oT_ready, t)
                for k in range(KT):
                    for half in range(2):
                        if half == 1:
                            pe.wait_ge(scores_masked, 2 * t + k + 1)
                        mm(b_o[:, k * P + half * HALF:k * P + (half + 1) * HALF], state_sb[:, half, k, :],
                           qT[:, k, half * HALF:(half + 1) * HALF], start=(half == 0 and k == 0), stop=False,
                           skip_group_check=True)

                def own_keys(half):
                    span = slice(half * HALF, (half + 1) * HALF)
                    for h in range(4):
                        for r in range(4):
                            at = h // 2 * P + half * HALF
                            last = mm(b_o[32 * r:32 * r + 32, at:at + HALF],
                                      v_pad[span, parity, h // 2 * 8 + 2 * r + h % 2, :], scores_sb[span, r, h, :],
                                      start=False, stop=True, skip_group_check=True)
                    return last

                own_keys(0).then_inc(own_done, 1)
                add_to_state(1, parity, lambda: pe.wait_ge(own_done, t + 1))
                own_keys(1).then_inc(o_ready, 1)

            project(0, 0, 1, None)
            pe.wait_ge(s_wout, 16)
            tile_loop(pe, step)
            output_projection(TILES - 1, TILES)

            pe.wait_ge(banks_zeroed, 1)
            for fc in range(2):
                with pe.Fori(0, ROUNDS) as n:
                    for s in range(SLOTS):
                        pe.wait_ge(slot_scaled, fc * PAIRS + n * SLOTS + s + 1)
                        if fc == 0:
                            for m in range(KT):
                                for c in range(2):
                                    last = mm(bank[2 * m + c], slot[:, s, m * P:(m + 1) * P],
                                              slot[:, s, DIM + c * 512:DIM + (c + 1) * 512],
                                              start=False, stop=True, skip_group_check=True)
                        else:
                            for f in range(FB):
                                last = mm(bank[4 + f // 2][:, (f % 2) * DIM:(f % 2 + 1) * DIM],
                                          slot[:, s, DIM + f * P:DIM + (f + 1) * P], slot[:, s, 0:DIM],
                                          start=False, stop=True, skip_group_check=True)
                        last.then_inc(slot_used, 1)

            def transpose_x1(g):
                pe.wait_ge(x1_copied, g + 1)
                for k in range(KT):
                    for j in range(GROUP):
                        last = nc.tensor.transpose(bank[4 + k][:, j * P:(j + 1) * P],
                                                   x1_group[:, j, k * P:(k + 1) * P], const("ident"))
                    last.then_inc(x1T_psum, 1)

            def group_step(g, has_next):
                pe.wait_ge(x1T_act, g + 1)
                pe.wait_ge(x1T_dve, g + 1)
                for f in range(FB):
                    if f >= RING:
                        pe.wait_ge(h_act, g * FB + f - RING + 1)
                    elif not (isinstance(g, int) and g == 0):
                        pe.wait_ge(h_act, g * FB + f - RING + 1)
                    for k in range(KT):
                        last = mm(bank[f % RING], w1_sb[:, k, f * P:(f + 1) * P], x1T[:, k, :],
                                  start=(k == 0), stop=(k == KT - 1))
                    last.then_inc(h_psum, 1)
                if has_next:
                    transpose_x1(g + 1)
                for j in range(GROUP):
                    n = g * GROUP + j
                    if j >= 2:
                        pe.wait_ge(y2_added, n - 1)
                    elif not (isinstance(g, int) and g == 0):
                        pe.wait_ge(y2_added, n - 1)
                    for f in range(FB):
                        if j == 0:
                            pe.wait_ge(h_act, g * FB + f + 1)
                        last = mm(bank[6 + j % 2][:, 0:DIM], hT[:, f, j * P:(j + 1) * P], w2_sb[:, f, :],
                                  start=(f == 0), stop=(f == FB - 1))
                    last.then_inc(y2_psum, 1)

            pe.wait_ge(w1_act, 2)
            pe.wait_ge(w1_dve, 2)
            pe.wait_ge(w2_act, 2)
            pe.wait_ge(w2_dve, 2)
            transpose_x1(0)
            group_step(0, True)
            with pe.Fori(1, GROUPS - 1) as g:
                group_step(g, True)
            group_step(GROUPS - 1, False)


def shape_constants():
    import numpy as np
    cols, ncols = const_columns()
    c = np.zeros((P, ncols), np.float32)
    i = np.arange(P)
    c[:, slice(*cols["tri"])] = i[:, None] <= i[None, :]
    c[:, slice(*cols["tri_rest"])] = i[:, None] > i[None, :]
    c[:, slice(*cols["score_mask"])] = (i[:, None] % HALF) <= i[None, :HALF]
    c[:, slice(*cols["head_mask"])] = (i[:, None] // HD) == (i[None, :] // HD)
    c[:, slice(*cols["ident"])] = i[:, None] == i[None, :]
    c[:, cols["even"][0]] = i // HD % 2 == 0
    c[:, cols["odd"][0]] = i // HD % 2 == 1
    half = HD // 2
    exps = np.arange(half, dtype=np.float32) / np.float32(half)
    inv_freq = np.float32(1.0) / np.power(np.float32(10000.0), exps)
    angle = np.arange(SEQ, dtype=np.float32)[:, None] * inv_freq[None, :]
    scale = np.float32(HD ** -0.25)
    cos, sin = np.cos(angle) * scale, np.sin(angle) * scale
    rope = np.concatenate([cos, cos, -sin, sin], axis=1).astype(np.float32)
    sel = np.zeros((2, 4, P), np.float32)
    for fc in range(2):
        for par in range(2):
            sel[fc, 2 * fc + par, par * RANK:(par + 1) * RANK] = 1.0
    return c, rope.reshape(TILES_PER_SEQ, P, 2 * HD), sel


def kernel(L0_attn_x, L0_attn_w_qkv, L0_attn_w_out, L0_ffn_fc1_A, L0_ffn_fc1_B, L0_ffn_fc2_A, L0_ffn_fc2_B,
           L0_ffn_fc1_logits, L0_ffn_fc2_logits):
    import numpy as np
    import concourse.bacc as bacc
    from concourse.bass_utils import run_bass_kernel_spmd

    consts, rope, sel = shape_constants()
    x = np.ascontiguousarray(np.asarray(L0_attn_x)).reshape(TILES * P, DIM)
    xT = x.reshape(TILES, P, KT, P).transpose(0, 3, 2, 1).reshape(TILES, P, DIM)
    xin = np.concatenate([xT, np.tile(rope, (BATCH, 1, 1))], axis=2)
    a1, b1 = np.asarray(L0_ffn_fc1_A), np.asarray(L0_ffn_fc1_B)
    a2, b2 = np.asarray(L0_ffn_fc2_A), np.asarray(L0_ffn_fc2_B)
    arrays = {
        "xin": np.ascontiguousarray(xin),
        "x": x,
        "w_qkv": np.ascontiguousarray(np.asarray(L0_attn_w_qkv)),
        "w_out": np.ascontiguousarray(np.asarray(L0_attn_w_out)),
        "consts": consts,
        "selectors": sel,
        "logits": np.stack([np.asarray(L0_ffn_fc1_logits), np.asarray(L0_ffn_fc2_logits)]),
        "factors1": np.ascontiguousarray(np.concatenate([a1.transpose(0, 2, 1), b1], axis=2)),
        "factors2": np.ascontiguousarray(np.concatenate([b2, a2.transpose(0, 2, 1)], axis=2)),
    }
    nc = bacc.Bacc("TRN2", target_bir_lowering=False, num_devices=1)
    ap = {n: nc.dram_tensor(n, a.shape, mybir.dt.from_np(a.dtype), kind="ExternalInput").ap() for n, a in arrays.items()}
    out = nc.dram_tensor("out", (TILES * P, DIM), F32, kind="ExternalOutput").ap()
    build_program(nc, ap["xin"], ap["x"], ap["w_qkv"], ap["w_out"], ap["consts"], ap["selectors"], ap["logits"],
                  (ap["factors1"], ap["factors2"]), out)
    r = run_bass_kernel_spmd(nc, [arrays], core_ids=[0])
    return r.results[0]["out"].reshape(BATCH, SEQ, DIM)
```

```python
from contextlib import ExitStack

import concourse.bass as bass
from concourse import mybir

F32 = mybir.dt.float32
F32R = mybir.dt.float32r
U32 = mybir.dt.uint32
ALU = mybir.AluOpType
ACT = mybir.ActivationFunctionType
AX = mybir.AxisListType

P = 128
BATCH, SEQ, DIM = 8, 1024, 256
HEADS, HD = 16, 16
HALF = 64
TILES = BATCH * SEQ // P
TILES_PER_SEQ = SEQ // P
KT = DIM // P
FFN = 1024
PRIMS, TOPK, RANK = 64, 32, 64
PAIRS = TOPK // 2
SLOTS = 4
ROUNDS = PAIRS // SLOTS
GROUP = 4
GROUPS = TILES // GROUP
FB = FFN // P
RING = 4
SPLITS = 2
LN_EPS = 1e-5
DEN_MIN = 1e-6
NEG = -3.0e38
CONSTS = dict(tri=P, tri_rest=P, score_mask=HALF, head_mask=P, ident=P, even=1, odd=1)


def const_columns():
    at, out = 0, {}
    for name, n in CONSTS.items():
        out[name] = (at, at + n)
        at += n
    return out, at


def build_program(nc, xin, x, w_qkv, w_out, consts, selectors, logits, factors, out):
    with ExitStack() as ctx:
        def sb(name, shape, dt=F32):
            return ctx.enter_context(nc.sbuf_tensor(name, shape, dt))

        def sem(name):
            return ctx.enter_context(nc.semaphore(name))

        psum = ctx.enter_context(nc.psum_tensor("psum", [P, 8, 512], F32))
        bank = [psum[:, i, :] for i in range(8)]

        stream = sb("stream", [P, TILES, DIM])
        cols, ncols = const_columns()
        const_sb = sb("const_sb", [P, ncols])

        def const(name):
            return const_sb[:, cols[name][0]:cols[name][1]]

        wqkv_hl = sb("wqkv_hl", [P, 2, KT, 3 * DIM], F32R)
        wout_hl = sb("wout_hl", [P, 2, KT, DIM], F32R)
        logit_sb = sb("logit_sb", [2, PRIMS])
        top_val = sb("top_val", [2, TOPK])
        top_idx = sb("top_idx", [2, TOPK], U32)
        neg_max = sb("neg_max", [2, 1])
        top_exp = sb("top_exp", [2, TOPK])
        top_sum = sb("top_sum", [2, 1])
        top_inv = sb("top_inv", [2, 1])
        top_w = sb("top_w", [2, TOPK])
        factor_w = sb("factor_w", [P, 2, PAIRS])
        xin_sb = sb("xin_sb", [P, 2, DIM + 2 * HD])
        scratch = sb("scratch", [P, 5, 2 * DIM])
        rope_cos, rope_sin, roped, feat_exp, feat_relu = (scratch[:, i] for i in range(5))
        sel_sb = scratch[0:2, 4].rearrange("a (b c) -> a b c", b=4)
        feat = sb("feat", [P, 2, 2 * DIM])
        v_pad = sb("v_pad", [P, 2, HEADS, 2 * HD])
        den_prod = sb("den_prod", [P, DIM])
        den = sb("den", [P, HEADS])
        den_max = sb("den_max", [P, HEADS])
        den_inv = sb("den_inv", [P, HEADS])
        q_norm = sb("q_norm", [P, DIM])
        qT = sb("qT", [P, KT, P])
        kT = sb("kT", [P, 2, KT, P])
        state_sb = sb("state_sb", [P, 2, KT, P])
        scores_sb = sb("scores_sb", [P, 4, 4, HALF])
        oT = sb("oT", [P, KT, P])
        fence_out = sb("fence_out", [P, 1])
        stats1 = sb("stats1", [P, TILES, 6])
        mean1 = sb("mean1", [P, TILES])
        moment_sum, moment_dif, moment_m2, moment_var, moment_sq = (
            scratch[:, 4, i * TILES:(i + 1) * TILES] for i in range(5))
        var1 = sb("var1", [P, TILES])
        exponent = sb("exponent", [P, TILES])
        rstd1 = sb("rstd1", [P, TILES])
        slot = sb("slot", [P, SLOTS, DIM + FFN])
        raw = slot[:, 2:4].rearrange("p a b -> p (a b)")
        raw_qkv = raw[:, 0:KT * 3 * DIM]
        raw_out = raw[:, KT * 3 * DIM:KT * 4 * DIM]
        split_store = sb("split_store", [P, 2 * FB * GROUP * P], F32R)
        factor_hl = split_store[:, 0:2 * SPLITS * (DIM + FFN)].rearrange("p (a s c) -> p a s c", a=2, s=SPLITS)
        xo = split_store[:, 2 * SPLITS * (DIM + FFN):][:, 0:6 * DIM].rearrange("p (a n) -> p a n", n=DIM)
        xT_high, xT_low = xo[:, 0:2], xo[:, 2:4]
        oT_high, oT_low = (xo[:, i].rearrange("p (k n) -> p k n", k=KT) for i in (4, 5))
        hT_hl = split_store[:].rearrange("p (a f n) -> p a f n", a=2, f=FB)
        w1_hl = sb("w1_hl", [P, 2, KT, FFN], F32R)
        w2_hl = sb("w2_hl", [P, 2, FB, DIM], F32R)
        gelu_out = scratch[:, 0:2]
        x1_group = scratch[:, 2:4].rearrange("p a b -> p (a b)").rearrange("p (t d) -> p t d", t=GROUP)
        x1T_hl = wqkv_hl[:].rearrange("p a k n -> p (a k n)")[:, 0:2 * KT * GROUP * P]\
            .rearrange("p (a k n) -> p a k n", a=2, k=KT)
        stats2 = sb("stats2", [P, GROUP, 6])
        mean2 = sb("mean2", [P, GROUP])
        var2 = sb("var2", [P, GROUP])
        rstd2 = sb("rstd2", [P, GROUP])

        b_qk, b_y, b_acc, b_o = bank[0:4]
        b_ksum, b_state = b_acc[:, 0:DIM], b_acc[:, DIM:2 * DIM]
        b_v = b_o[:, DIM:2 * DIM]
        b_scores = psum[:, 4:8, :]
        b_kT, b_qT = bank[6][:, 0:DIM], bank[7][:, 0:DIM]

        def flat(a):
            return a.rearrange("p a d -> p (a d)")

        s_logits, s_const, s_sel, s_wqkv, s_wout = (sem(n) for n in (
            "logits_loaded", "const_loaded", "sel_loaded", "wqkv_loaded", "wout_loaded"))
        s_xin = [sem("xin_loaded0"), sem("xin_loaded1")]
        s_res = [sem("residual_loaded0"), sem("residual_loaded1")]
        s_slot = [sem(f"slot_loaded{s}") for s in range(SLOTS)]
        (topk_step, topk_done, top_exp_done, top_w_done, bcast_ready, factor_w_ready, zeroed, w_high, w_low) = (
            sem(n) for n in ("topk_step", "topk_done", "top_exp_done", "top_w_done", "bcast_ready",
                             "factor_w_ready", "zeroed", "w_high", "w_low"))
        (x_high, x_low, qk_ready, v_ready, qk_used, v_used, roped_ready, exp_done, relu_done, feat_ready,
         carry_ready, ksum_ready, ksum_used, den_done, den_max_done, den_inv_done, qnorm_ready,
         state_ready, mid_ready, acc_done, own_done, kT_psum, qT_psum, kT_ready, qT_ready, scores_ready,
         scores_masked, o_ready, o_high, o_used, o_low, y_ready, y_used, stats1_ready) = (sem(n) for n in (
             "x_high", "x_low", "qk_ready", "v_ready", "qk_used", "v_used", "roped_ready", "exp_done", "relu_done",
             "feat_ready", "carry_ready", "ksum_ready", "ksum_used", "den_done", "den_max_done", "den_inv_done",
             "qnorm_ready", "state_ready", "mid_ready", "acc_done", "own_done", "kT_psum", "qT_psum",
             "kT_ready", "qT_ready", "scores_ready", "scores_masked", "o_ready", "o_high", "o_used", "o_low",
             "y_ready", "y_used", "stats1_ready"))
        (factor_high, factor_low, pair_summed, banks_zeroed, moment_step, w1_high, w1_low, w2_high, w2_low, var1_ready,
         rstd1_ready) = (sem(n) for n in (
             "factor_high", "factor_low", "pair_summed", "banks_zeroed", "moment_step", "w1_high", "w1_low",
             "w2_high", "w2_low", "var1_ready", "rstd1_ready"))
        (x1_ready, x1_copied, x1T_psum, x1T_high, x1T_low, h_psum, h_act, h_high, h_low, y2_psum, y2_added,
         stats2_ready, var2_ready, rstd2_ready, result_ready, stored) = (sem(n) for n in (
             "x1_ready", "x1_copied", "x1T_psum", "x1T_high", "x1T_low", "h_psum", "h_act", "h_high",
             "h_low", "y2_psum", "y2_added", "stats2_ready", "var2_ready", "rstd2_ready", "result_ready",
             "stored"))

        block = ctx.enter_context(nc.Block())

        def tile_loop(engine, step):
            step(0, 0, 2)
            with engine.Fori(1, TILES // 2 - 1) as i:
                step(2 * i - 1, 1, i + 1)
                step(2 * i, 0, i + 2)
            for t in range(TILES - 3, TILES):
                step(t, t % 2, t // 2 + 2)

        def at(t, least):
            return t >= least if isinstance(t, int) else least <= 1

        def before(t, end):
            return t < end if isinstance(t, int) else True

        def starts_late(g):
            return not isinstance(g, int) or g > 0

        @block.sync
        def _(sp):
            tokens = x.rearrange("(t p) d -> t p d", p=P)

            def load_tile(t, p):
                sp.dma_start(xin_sb[:, p, :], xin[bass.ds(t, 1)].rearrange("a p c -> (a p) c")).then_inc(s_xin[p], 16)
                sp.dma_start(flat(stream[:, bass.ds(t, 1), :]), tokens[bass.ds(t, 1)].rearrange("a p c -> (a p) c"))\
                    .then_inc(s_res[p], 16)

            sp.dma_start(raw_qkv.rearrange("p (k n) -> p k n", k=KT), w_qkv.rearrange("(k p) n -> p k n", p=P))\
                .then_inc(s_wqkv, 16)
            load_tile(0, 0)
            sp.dma_start(const_sb[:], consts).then_inc(s_const, 16)
            load_tile(1, 1)
            sp.dma_start(raw_out.rearrange("p (k n) -> p k n", k=KT), w_out.rearrange("(k p) n -> p k n", p=P))\
                .then_inc(s_wout, 16)
            sp.dma_start(logit_sb[:], logits).then_inc(s_logits, 16)
            sp.dma_start(sel_sb, selectors).then_inc(s_sel, 16)

            def gather(fc, n, s, first):
                if not first:
                    sp.wait_ge(factor_low, fc * PAIRS + n - SLOTS + 1)
                for half in range(2):
                    k = sp.value_load(top_idx[fc:fc + 1, bass.ds(2 * n + half, 1)], min_val=0, max_val=PRIMS - 1)
                    sp.dma_start(slot[half * RANK:(half + 1) * RANK, s, :],
                                 factors[fc][bass.ds(k, 1)].rearrange("a r c -> (a r) c")).then_inc(s_slot[s], 16)

            sp.wait_ge(topk_done, 1)
            sp.wait_ge(w_low, 2)
            for s in range(SLOTS):
                gather(0, s, s, True)

            def next_tile(t, p):
                sp.wait_ge(x_low, t - 1)
                sp.wait_ge(qk_used, t - 1)
                load_tile(t, p)

            with sp.Fori(1, TILES // 2) as i:
                next_tile(2 * i, 0)
                next_tile(2 * i + 1, 1)
            with sp.Fori(1, ROUNDS) as r:
                for s in range(SLOTS):
                    gather(0, r * SLOTS + s, s, False)
            with sp.Fori(0, ROUNDS) as r:
                for s in range(SLOTS):
                    gather(1, r * SLOTS + s, s, False)
            result_out = out.rearrange("(g t p) d -> g p t d", t=GROUP, p=P)

            def copy_x1(g):
                sp.wait_ge(x1_ready, (g + 1) * GROUP)
                if starts_late(g):
                    sp.wait_ge(x1T_psum, 2 * g)
                sp.dma_start(x1_group, stream[:, bass.ds(g * GROUP, GROUP), :]).then_inc(x1_copied, 16)

            def group_step(g, has_next):
                if has_next:
                    copy_x1(g + 1)
                sp.wait_ge(result_ready, g + 1)
                sp.dma_start(result_out[bass.ds(g, 1)].rearrange("a p t d -> p (a t) d"),
                             stream[:, bass.ds(g * GROUP, GROUP), :]).then_inc(stored, 16)

            copy_x1(0)
            group_step(0, True)
            with sp.Fori(1, GROUPS - 1) as g:
                group_step(g, True)
            group_step(GROUPS - 1, False)
            sp.wait_ge(stored, 16 * GROUPS)

        @block.gpsimd
        def _(pool):
            def rope_sum(n):
                pool.wait_ge(qk_used, n + 1)
                if at(n, 1):
                    pool.wait_ge(relu_done, n)
                nc.gpsimd.tensor_tensor(roped, rope_cos, rope_sin, ALU.add).then_inc(roped_ready, 1)

            def split_x(n, p):
                pool.wait_ge(x_high, n + 1)
                nc.gpsimd.tensor_tensor(xT_low[:, p], xin_sb[:, p, 0:DIM], xT_high[:, p].bitcast(F32),
                                        ALU.subtract).then_inc(x_low, 1)

            def split_o(n):
                pool.wait_ge(o_used, n + 1)
                if at(n, 1):
                    pool.wait_ge(y_ready, n)
                nc.gpsimd.tensor_tensor(oT_low, oT[:], oT_high.bitcast(F32), ALU.subtract).then_inc(o_low, 1)

            def step(t, parity, uses):
                if at(t, 1):
                    split_o(t - 1)
                if before(t, TILES - 2):
                    split_x(t + 2, parity)
                if before(t, TILES - 1):
                    rope_sum(t + 1)

            nc.gpsimd.memset(v_pad[:], 0.0).then_inc(zeroed, 1)
            nc.gpsimd.memset(exponent[:], -0.5).then_inc(zeroed, 1)
            split_x(0, 0)
            split_x(1, 1)
            rope_sum(0)
            tile_loop(pool, step)
            split_o(TILES - 1)
            pool.wait_ge(var1_ready, 1)
            pool.wait_ge(zeroed, 2)
            nc.gpsimd.tensor_tensor(rstd1[:], var1[:], exponent[:], ALU.pow).then_inc(rstd1_ready, 1)
            with pool.Fori(0, GROUPS) as g:
                pool.wait_ge(var2_ready, g + 1)
                nc.gpsimd.tensor_tensor(rstd2[:], var2[:], exponent[:, 0:GROUP], ALU.pow).then_inc(rstd2_ready, 1)

        @block.scalar
        def _(act):
            copy = nc.scalar.activation

            def split_x(n, p, loads):
                act.wait_ge(s_xin[p], 16 * loads)
                if at(n, 2) and not (isinstance(n, int) and n < 2):
                    act.wait_ge(v_ready, n - 1)
                copy(xT_high[:, p], xin_sb[:, p, 0:DIM], ACT.Copy).then_inc(x_high, 1)

            def move_v(n, p):
                act.wait_ge(v_ready, n + 1)
                if isinstance(n, int) and n < 2:
                    act.wait_ge(zeroed, 2)
                dst = v_pad[:, p].rearrange("k (a b) c -> k a (b c)", b=2)
                dst = dst.rearrange("k a (b c) -> k a b c", c=HD)[:, :, 0:4:3, :]
                copy(dst, b_v.rearrange("k (a b c) -> k a b c", b=2, c=HD), ACT.Copy).then_inc(v_used, 1)

            def features(n):
                act.wait_ge(roped_ready, n + 1)
                if at(n, 1):
                    act.wait_ge(feat_ready, n)
                copy(feat_exp, roped, ACT.Exp).then_inc(exp_done, 1)
                copy(feat_relu, roped, ACT.Relu).then_inc(relu_done, 1)

            def move_o(n):
                act.wait_ge(o_ready, n + 1)
                if at(n, 1):
                    act.wait_ge(y_ready, n)
                o = b_o[:, 0:DIM].rearrange("p (k n) -> p k n", k=KT)
                copy(oT_high, o, ACT.Copy).then_inc(o_high, 1)
                copy(oT[:], o, ACT.Copy).then_inc(o_used, 1)

            def step(t, parity, uses):
                if at(t, 1):
                    move_o(t - 1)
                act.wait_ge(kT_psum, t + 1)
                k = b_kT.rearrange("p (k n) -> p k n", k=KT)
                copy(kT[:, 0], k, ACT.Copy, scale=const("even")).then_inc(kT_ready, 1)
                copy(kT[:, 1], k, ACT.Copy, scale=const("odd")).then_inc(kT_ready, 1)
                if before(t, TILES - 2):
                    split_x(t + 2, parity, uses)
                act.wait_ge(qT_psum, t + 1)
                copy(qT[:], b_qT.rearrange("p (k n) -> p k n", k=KT), ACT.Copy).then_inc(qT_ready, 1)
                if before(t, TILES - 1):
                    move_v(t + 1, 1 - parity)
                    features(t + 1)

            split_x(0, 0, 1)
            act.wait_ge(s_wqkv, 16)
            copy(wqkv_hl[:, 0].rearrange("p k n -> p (k n)"), raw_qkv, ACT.Copy).then_inc(w_high, 1)
            split_x(1, 1, 1)
            act.wait_ge(s_wout, 16)
            copy(wout_hl[:, 0].rearrange("p k n -> p (k n)"), raw_out, ACT.Copy).then_inc(w_high, 1)
            act.wait_ge(s_const, 16)
            move_v(0, 0)
            act.wait_ge(topk_done, 1)
            nc.scalar.activation(top_exp[:], top_val[:], ACT.Exp, bias=neg_max[:, 0:1],
                                 accum_out=top_sum[:]).then_inc(top_exp_done, 1)
            act.wait_ge(bcast_ready, 1)
            features(0)
            tile_loop(act, step)
            move_o(TILES - 1)

            def split_factors(fc, n, s):
                act.wait_ge(s_slot[s], 32 * (fc * ROUNDS + n + 1))
                pair = fc * PAIRS + n * SLOTS + s
                if not (isinstance(n, int) and fc == 0 and n == 0 and s < SPLITS):
                    act.wait_ge(pair_summed, pair - SPLITS + 1)
                copy(factor_hl[:, 0, s % SPLITS, DIM:], slot[:, s, DIM:], ACT.Copy)
                copy(factor_hl[:, 0, s % SPLITS, 0:DIM], slot[:, s, 0:DIM], ACT.Copy,
                     scale=factor_w[:, fc, bass.ds(n * SLOTS + s, 1)]).then_inc(factor_high, 1)

            act.wait_ge(factor_w_ready, 1)
            for s in range(SLOTS):
                split_factors(0, 0, s)
            with act.Fori(1, ROUNDS) as n:
                for s in range(SLOTS):
                    split_factors(0, n, s)
            act.wait_ge(pair_summed, PAIRS)
            for k in range(KT):
                copy(w1_hl[:, 0, k, :].rearrange("p (c n) -> p c n", c=2), psum[:, 2 * k:2 * k + 2, :], ACT.Copy)\
                    .then_inc(w1_high, 1)
            with act.Fori(0, ROUNDS) as n:
                for s in range(SLOTS):
                    split_factors(1, n, s)
            act.wait_ge(pair_summed, 2 * PAIRS)
            for k in range(2):
                copy(w2_hl[:, 0, 4 * k:4 * k + 4, :].rearrange("p (c f) n -> p c (f n)", c=2),
                     psum[:, 4 + 2 * k:6 + 2 * k, :], ACT.Copy).then_inc(w2_high, 1)

            def move_x1T(g):
                for k in range(KT):
                    act.wait_ge(x1T_psum, 2 * g + k + 1)
                    copy(x1T_hl[:, 0, k, :], bank[4 + k], ACT.Copy).then_inc(x1T_high, 1)

            def group_step(g, has_next):
                for f in range(FB):
                    act.wait_ge(h_psum, g * FB + f + 1)
                    if f >= 2 or starts_late(g):
                        act.wait_ge(h_low, g * FB + f - 1)
                    copy(gelu_out[:, f % 2], bank[f % RING], ACT.Gelu_apprx_tanh).then_inc(h_act, 1)
                if has_next:
                    move_x1T(g + 1)

            move_x1T(0)
            group_step(0, True)
            with act.Fori(1, GROUPS - 1) as g:
                group_step(g, True)
            group_step(GROUPS - 1, False)

        @block.vector
        def _(dve):
            steps = [0]

            def chained(instruction):
                steps[0] += 1
                instruction.then_inc(topk_step, 1)
                dve.wait_ge(topk_step, steps[0])

            for n, (raw_w, hl, loaded) in enumerate(((raw_qkv, wqkv_hl, s_wqkv), (raw_out, wout_hl, s_wout))):
                dve.wait_ge(loaded, 16)
                dve.wait_ge(w_high, n + 1)
                high, low = (hl[:, i].rearrange("p k n -> p (k n)") for i in range(2))
                nc.vector.tensor_tensor(low, raw_w, high.bitcast(F32), ALU.subtract).then_inc(w_low, 1)
            dve.wait_ge(s_const, 16)

            def rope(n, p):
                dve.wait_ge(qk_ready, n + 1)
                if at(n, 1):
                    dve.wait_ge(roped_ready, n)
                qk = b_qk.rearrange("p (h c) -> p h c", c=HD)
                cos = xin_sb[:, p, DIM:DIM + HD].unsqueeze(1).broadcast_to([P, 2 * HEADS, HD])
                nc.vector.tensor_tensor(rope_cos.rearrange("p (h c) -> p h c", c=HD), qk, cos, ALU.mult)
                sin = xin_sb[:, p, DIM + HD:DIM + 2 * HD]
                half = HD // 2
                nc.vector.tensor_tensor(
                    rope_sin.rearrange("p (h c) -> p h c", c=HD)[:, :, 0:half], qk[:, :, half:HD],
                    sin[:, 0:half].unsqueeze(1).broadcast_to([P, 2 * HEADS, half]), ALU.mult)
                nc.vector.tensor_tensor(
                    rope_sin.rearrange("p (h c) -> p h c", c=HD)[:, :, half:HD], qk[:, :, 0:half],
                    sin[:, half:HD].unsqueeze(1).broadcast_to([P, 2 * HEADS, half]), ALU.mult).then_inc(qk_used, 1)

            def finish_features(n, p):
                dve.wait_ge(exp_done, n + 1)
                dve.wait_ge(relu_done, n + 1)
                nc.vector.scalar_tensor_tensor(out=feat[:, p, :], in0=feat_exp, scalar=1.0, in1=feat_relu,
                                               op0=ALU.min, op1=ALU.add).then_inc(feat_ready, 1)

            def mask_state(which):
                return nc.vector.tensor_tensor(
                    state_sb[:, which], b_state.rearrange("p (k n) -> p k n", k=KT),
                    const("head_mask").unsqueeze(1).broadcast_to([P, KT, P]), ALU.mult)

            def carry(t, new_sequence):
                if at(t, 1):
                    dve.wait_ge(state_ready, 2 * t)
                if new_sequence is True:
                    nc.vector.memset(b_acc, 0.0).then_inc(topk_step, 1)
                    dve.wait_ge(topk_step, steps[0] + 1)
                elif new_sequence is not None:
                    with dve.If_eq(dve.to_reg(new_sequence % (TILES_PER_SEQ // 2)), 0):
                        nc.vector.memset(b_acc, 0.0)
                        nc.vector.drain()
                mask_state(0).then_inc(carry_ready, 1)

            def fence(semaphore, value):
                dve.wait_ge(semaphore, value)
                nc.vector.tensor_copy(fence_out[:], const("even"))

            def moments(stats, n, base, mean, var, signal):
                v = nc.vector
                v.tensor_tensor(moment_sum[:, 0:n], stats[:, :, 1], stats[:, :, 4], ALU.add)
                v.tensor_tensor(moment_dif[:, 0:n], stats[:, :, 1], stats[:, :, 4], ALU.subtract)
                v.tensor_tensor(moment_m2[:, 0:n], stats[:, :, 2], stats[:, :, 5], ALU.add).then_inc(moment_step, 1)
                dve.wait_ge(moment_step, base + 1)
                v.tensor_scalar(mean[:], moment_sum[:, 0:n], 0.5, None, ALU.mult)
                v.tensor_tensor(moment_sq[:, 0:n], moment_dif[:, 0:n], moment_dif[:, 0:n], ALU.mult)
                v.tensor_scalar(moment_var[:, 0:n], moment_m2[:, 0:n], 1.0 / DIM, LN_EPS, ALU.mult, ALU.add)\
                    .then_inc(moment_step, 1)
                dve.wait_ge(moment_step, base + 2)
                v.scalar_tensor_tensor(out=var[:], in0=moment_sq[:, 0:n], scalar=0.25, in1=moment_var[:, 0:n],
                                       op0=ALU.mult, op1=ALU.add).then_inc(signal, 1)

            def layer_norm1(n, p, loads):
                dve.wait_ge(s_res[p], 16 * loads)
                dve.wait_ge(y_ready, n + 1)
                row = flat(stream[:, bass.ds(n, 1), :])
                nc.vector.tensor_tensor(row, b_y[:, 0:DIM], row, ALU.add).then_inc(y_used, 1)
                fence(y_used, n + 1)
                nc.vector.bn_stats(flat(stats1[:, bass.ds(n, 1), :]), row).then_inc(stats1_ready, 1)

            def step(t, parity, uses):
                if isinstance(t, int):
                    carry(t, True if t == 0 else None)
                else:
                    carry(t, uses - 2 if parity == 0 else None)
                dve.wait_ge(ksum_ready, t + 1)
                nc.vector.tensor_tensor(den_prod[:], feat[:, parity, 0:DIM], b_ksum, ALU.mult).then_inc(ksum_used, 1)
                dve.wait_ge(ksum_used, t + 1)
                nc.vector.tensor_reduce(den[:], den_prod[:].rearrange("p (h c) -> p h c", c=HD), AX.X, ALU.add)\
                    .then_inc(den_done, 1)
                dve.wait_ge(den_done, t + 1)
                nc.vector.tensor_scalar(den_max[:], den[:], DEN_MIN, None, ALU.max).then_inc(den_max_done, 1)
                dve.wait_ge(den_max_done, t + 1)
                nc.vector.reciprocal(den_inv[:], den_max[:]).then_inc(den_inv_done, 1)
                dve.wait_ge(den_inv_done, t + 1)
                nc.vector.tensor_tensor(q_norm[:].rearrange("p (h c) -> p h c", c=HD),
                                        feat[:, parity, 0:DIM].rearrange("p (h c) -> p h c", c=HD),
                                        den_inv[:].unsqueeze(2).broadcast_to([P, HEADS, HD]), ALU.mult).then_inc(qnorm_ready, 1)
                if before(t, TILES - 1):
                    rope(t + 1, 1 - parity)
                if at(t, 1):
                    layer_norm1(t - 1, 1 - parity, uses - 1 if parity == 1 else uses - 2)
                dve.wait_ge(state_ready, 2 * t + 1)
                mask_state(1).then_inc(mid_ready, 1)
                for part in range(2):
                    dve.wait_ge(scores_ready, 2 * t + part + 1)
                    tiles = slice(2 * part, 2 * part + 2)
                    nc.vector.tensor_tensor(
                        scores_sb[:, tiles], b_scores[:, tiles, 0:4 * HALF].rearrange("p r (h q) -> p r h q", h=4),
                        const("score_mask").unsqueeze(1).unsqueeze(1).broadcast_to([P, 2, 4, HALF]),
                        ALU.mult).then_inc(scores_masked, 1)
                if before(t, TILES - 1):
                    finish_features(t + 1, 1 - parity)

            rope(0, 0)
            steps = [0]

            def chained(instruction):
                steps[0] += 1
                instruction.then_inc(topk_step, 1)
                dve.wait_ge(topk_step, steps[0])

            dve.wait_ge(s_logits, 16)
            for r in range(TOPK // 8):
                eight = slice(8 * r, 8 * r + 8)
                chained(nc.vector.max(top_val[:, eight], logit_sb[:]))
                chained(nc.vector.max_index(top_idx[:, eight], top_val[:, eight], logit_sb[:]))
                if r < TOPK // 8 - 1:
                    chained(nc.vector.match_replace(logit_sb[:], top_val[:, eight], logit_sb[:], NEG))
            nc.vector.tensor_scalar(neg_max[:], top_val[:, 0:1], -1.0, None, ALU.mult).then_inc(topk_done, 1)
            dve.wait_ge(top_exp_done, 1)
            chained(nc.vector.reciprocal(top_inv[:], top_sum[:]))
            nc.vector.tensor_scalar(top_w[:], top_exp[:], top_inv[:, 0:1], None, ALU.mult).then_inc(top_w_done, 1)
            dve.wait_ge(bcast_ready, 1)
            nc.vector.tensor_copy(factor_w[:], b_o[:, 0:2 * PAIRS].rearrange("p (f n) -> p f n", f=2))\
                .then_inc(factor_w_ready, 1)
            finish_features(0, 0)
            tile_loop(dve, step)
            layer_norm1(TILES - 1, 1, TILES // 2)
            dve.wait_ge(stats1_ready, TILES)
            moments(stats1, TILES, 0, mean1, var1, var1_ready)

            dve.wait_ge(o_used, TILES)
            for b in bank:
                last = nc.vector.memset(b, 0.0)
            last.then_inc(banks_zeroed, 1)

            def split_factors(fc, n, s):
                pair = fc * PAIRS + n * SLOTS + s
                dve.wait_ge(s_slot[s], 32 * (fc * ROUNDS + n + 1))
                dve.wait_ge(factor_high, pair + 1)
                high, low = factor_hl[:, 0, s % SPLITS], factor_hl[:, 1, s % SPLITS]
                nc.vector.tensor_tensor(low[:, DIM:], slot[:, s, DIM:], high[:, DIM:].bitcast(F32), ALU.subtract)
                nc.vector.scalar_tensor_tensor(out=low[:, 0:DIM], in0=slot[:, s, 0:DIM],
                                               scalar=factor_w[:, fc, bass.ds(n * SLOTS + s, 1)],
                                               in1=high[:, 0:DIM].bitcast(F32), op0=ALU.mult,
                                               op1=ALU.subtract).then_inc(factor_low, 1)

            for fc in range(2):
                with dve.Fori(0, ROUNDS) as n:
                    for s in range(SLOTS):
                        split_factors(fc, n, s)
                if fc == 0:
                    for k in range(KT):
                        dve.wait_ge(w1_high, k + 1)
                        high, low = (w1_hl[:, i, k, :].rearrange("p (c n) -> p c n", c=2) for i in range(2))
                        nc.vector.tensor_tensor(low, psum[:, 2 * k:2 * k + 2, :], high.bitcast(F32),
                                                ALU.subtract).then_inc(w1_low, 1)
            for k in range(2):
                dve.wait_ge(w2_high, k + 1)
                high, low = (w2_hl[:, i, 4 * k:4 * k + 4, :].rearrange("p (c f) n -> p c (f n)", c=2) for i in range(2))
                nc.vector.tensor_tensor(low, psum[:, 4 + 2 * k:6 + 2 * k, :], high.bitcast(F32),
                                        ALU.subtract).then_inc(w2_low, 1)

            dve.wait_ge(rstd1_ready, 1)

            def normalise1(g):
                for j in range(GROUP):
                    t = g * GROUP + j
                    row = stream[:, bass.ds(t, 1), :].rearrange("p a d -> p (a d)")
                    nc.vector.tensor_scalar(row, row, mean1[:, bass.ds(t, 1)],
                                            rstd1[:, bass.ds(t, 1)], ALU.subtract, ALU.mult).then_inc(x1_ready, 1)

            def split_x1T(g):
                for k in range(KT):
                    dve.wait_ge(x1T_high, 2 * g + k + 1)
                    nc.vector.tensor_tensor(x1T_hl[:, 1, k, :], bank[4 + k], x1T_hl[:, 0, k, :].bitcast(F32),
                                            ALU.subtract).then_inc(x1T_low, 1)

            def split_h(g, f):
                dve.wait_ge(h_act, g * FB + f + 1)
                if f == 0 and starts_late(g):
                    dve.wait_ge(y2_psum, g * GROUP)
                nc.vector.tensor_copy(hT_hl[:, 0, f, :], gelu_out[:, f % 2]).then_inc(h_high, 1)
                dve.wait_ge(h_high, g * FB + f + 1)
                nc.vector.tensor_tensor(hT_hl[:, 1, f, :], gelu_out[:, f % 2], hT_hl[:, 0, f, :].bitcast(F32),
                                        ALU.subtract).then_inc(h_low, 1)

            def group_step(g, has_next):
                for f in range(FB):
                    split_h(g, f)
                    if f == 1 and has_next:
                        normalise1(g + 1)
                if has_next:
                    split_x1T(g + 1)
                for j in range(GROUP):
                    n = g * GROUP + j
                    row = stream[:, bass.ds(n, 1), :].rearrange("p a d -> p (a d)")
                    dve.wait_ge(y2_psum, n + 1)
                    dve.wait_ge(x1_ready, n + 1)
                    nc.vector.tensor_tensor(row, bank[6 + j % 2][:, 0:DIM], row, ALU.add).then_inc(y2_added, 1)
                    fence(y2_added, n + 1)
                    nc.vector.bn_stats(stats2[:, j, :], row).then_inc(stats2_ready, 1)
                dve.wait_ge(stats2_ready, (g + 1) * GROUP)
                moments(stats2, GROUP, 2 + 2 * g, mean2, var2, var2_ready)
                dve.wait_ge(rstd2_ready, g + 1)
                for j in range(GROUP):
                    row = stream[:, bass.ds(g * GROUP + j, 1), :].rearrange("p a d -> p (a d)")
                    last = nc.vector.tensor_scalar(row, row, mean2[:, j:j + 1], rstd2[:, j:j + 1], ALU.subtract, ALU.mult)
                last.then_inc(result_ready, 1)

            normalise1(0)
            split_x1T(0)
            group_step(0, True)
            with dve.Fori(1, GROUPS - 1) as g:
                group_step(g, True)
            group_step(GROUPS - 1, False)

        @block.tensor
        def _(pe):
            mm = nc.tensor.matmul

            def split_product(to, left, right, start=True, first=True, last=True):
                terms = ((0, 0), (0, 1), (1, 0))
                for i, (a, b) in enumerate(terms):
                    product = mm(to, left[a], right[b], start=start and first and i == 0,
                                 stop=(last and i == 2) or not start, skip_group_check=not start)
                return product

            def project_qk(n, p):
                pe.wait_ge(x_high, n + 1)
                pe.wait_ge(x_low, n + 1)
                if at(n, 1):
                    pe.wait_ge(qk_used, n)
                for k in range(KT):
                    last = split_product(b_qk, (xT_high[:, p, k * P:(k + 1) * P], xT_low[:, p, k * P:(k + 1) * P]),
                                         (wqkv_hl[:, 0, k, 0:2 * DIM], wqkv_hl[:, 1, k, 0:2 * DIM]),
                                         first=(k == 0), last=(k == KT - 1))
                last.then_inc(qk_ready, 1)

            def project_v(n, p):
                if at(n, 1):
                    pe.wait_ge(v_used, n)
                    if not (isinstance(n, int) and n == 1):
                        pe.wait_ge(o_used, n - 1)
                for k in range(KT):
                    last = split_product(b_v, (xT_high[:, p, k * P:(k + 1) * P], xT_low[:, p, k * P:(k + 1) * P]),
                                         (wqkv_hl[:, 0, k, 2 * DIM:], wqkv_hl[:, 1, k, 2 * DIM:]),
                                         first=(k == 0), last=(k == KT - 1))
                last.then_inc(v_ready, 1)

            def output_projection(t):
                pe.wait_ge(o_high, t + 1)
                pe.wait_ge(o_low, t + 1)
                if at(t, 1):
                    pe.wait_ge(y_used, t)
                for k in range(KT):
                    last = split_product(b_y[:, 0:DIM], (oT_high[:, k, :], oT_low[:, k, :]),
                                         (wout_hl[:, 0, k, :], wout_hl[:, 1, k, :]), first=(k == 0), last=(k == KT - 1))
                last.then_inc(y_ready, 1)

            def add_to_state(half, parity, before_last=None):
                rows = slice(half * HALF, (half + 1) * HALF)
                values = v_pad[rows, parity].rearrange("k (a b) c -> k a (b c)", b=2)
                values = values.rearrange("k a (b c) -> k a b c", c=HD)[:, :, 0:4:3, :]
                for k in range(KT):
                    if k == KT - 1 and before_last is not None:
                        before_last()
                    last = mm(b_state[:, k * P:(k + 1) * P], feat[rows, parity, DIM + k * P:DIM + (k + 1) * P],
                              values[:, 4 * k:4 * k + 4], start=False, stop=True, skip_group_check=True)
                last.then_inc(state_ready, 1)

            def transpose(to, src):
                for k in range(KT):
                    last = nc.tensor.transpose(to[:, k * P:(k + 1) * P], src[:, k * P:(k + 1) * P], const("ident"))
                return last

            def step(t, parity, uses):
                pe.wait_ge(feat_ready, t + 1)
                pe.wait_ge(carry_ready, t + 1)
                mm(b_ksum, const("tri"), feat[:, parity, DIM:2 * DIM], start=False, stop=True,
                   skip_group_check=True).then_inc(ksum_ready, 1)
                transpose(b_kT, feat[:, parity, DIM:2 * DIM]).then_inc(kT_psum, 1)
                if before(t, TILES - 1):
                    project_qk(t + 1, 1 - parity)
                if at(t, 1):
                    output_projection(t - 1)
                pe.wait_ge(qnorm_ready, t + 1)
                transpose(b_qT, q_norm).then_inc(qT_psum, 1)
                if before(t, TILES - 1):
                    project_v(t + 1, 1 - parity)
                pe.wait_ge(ksum_used, t + 1)
                pe.wait_ge(v_used, t + 1)
                add_to_state(0, parity)
                pe.wait_ge(kT_ready, 2 * t + 2)
                pe.wait_ge(qT_ready, t + 1)
                for part in range(2):
                    for h in range(4):
                        for half in range(2):
                            span = slice(half * HALF, (half + 1) * HALF)
                            for r in (2 * part, 2 * part + 1):
                                rows = slice(32 * r, 32 * r + 32)
                                last = mm(b_scores[span, r, h * HALF:(h + 1) * HALF],
                                          kT[rows, h % 2, h // 2, span], qT[rows, h // 2, span], start=True, stop=True)
                    last.then_inc(scores_ready, 1)
                pe.wait_ge(mid_ready, t + 1)
                mm(b_ksum, const("tri_rest"), feat[:, parity, DIM:2 * DIM], start=False, stop=True,
                   skip_group_check=True).then_inc(acc_done, 1)
                if before(t, TILES - 1):
                    pe.wait_ge(v_used, t + 2)
                elif at(t, 1):
                    pe.wait_ge(o_used, t)
                for k in range(KT):
                    for half in range(2):
                        if half == 1:
                            pe.wait_ge(scores_masked, 2 * t + k + 1)
                        mm(b_o[:, k * P + half * HALF:k * P + (half + 1) * HALF], state_sb[:, half, k, :],
                           qT[:, k, half * HALF:(half + 1) * HALF], start=(half == 0 and k == 0), stop=False,
                           skip_group_check=True)

                def own_keys(half):
                    span = slice(half * HALF, (half + 1) * HALF)
                    for h in range(4):
                        for r in range(4):
                            column = h // 2 * P + half * HALF
                            last = mm(b_o[32 * r:32 * r + 32, column:column + HALF],
                                      v_pad[span, parity, h // 2 * 8 + 2 * r + h % 2, :], scores_sb[span, r, h, :],
                                      start=False, stop=True, skip_group_check=True)
                    return last

                own_keys(0).then_inc(own_done, 1)
                add_to_state(1, parity, lambda: pe.wait_ge(own_done, t + 1))
                own_keys(1).then_inc(o_ready, 1)

            pe.wait_ge(w_high, 2)
            pe.wait_ge(w_low, 2)
            project_qk(0, 0)
            project_v(0, 0)
            pe.wait_ge(s_sel, 16)
            pe.wait_ge(top_w_done, 1)
            pe.wait_ge(v_used, 1)
            for fc in range(2):
                for half in range(2):
                    last = mm(b_o[:, fc * PAIRS:(fc + 1) * PAIRS], sel_sb[:, 2 * fc + half, :], top_w[:, half:TOPK:2],
                              start=(half == 0), stop=(half == 1))
            last.then_inc(bcast_ready, 1)
            pe.wait_ge(factor_w_ready, 1)
            pe.wait_ge(s_const, 16)
            tile_loop(pe, step)
            output_projection(TILES - 1)

            pe.wait_ge(banks_zeroed, 1)
            for fc in range(2):
                with pe.Fori(0, ROUNDS) as n:
                    for s in range(SLOTS):
                        pe.wait_ge(factor_low, fc * PAIRS + n * SLOTS + s + 1)
                        part = [factor_hl[:, i, s % SPLITS] for i in range(2)]
                        if fc == 0:
                            for m in range(KT):
                                for c in range(2):
                                    last = split_product(bank[2 * m + c], [a[:, m * P:(m + 1) * P] for a in part],
                                                         [a[:, DIM + c * 512:DIM + (c + 1) * 512] for a in part],
                                                         start=False)
                        else:
                            for f in range(FB):
                                last = split_product(bank[4 + f // 2][:, (f % 2) * DIM:(f % 2 + 1) * DIM],
                                                     [a[:, DIM + f * P:DIM + (f + 1) * P] for a in part],
                                                     [a[:, 0:DIM] for a in part], start=False)
                        last.then_inc(pair_summed, 1)

            def transpose_x1(g):
                pe.wait_ge(x1_copied, 16 * (g + 1))
                for k in range(KT):
                    for j in range(GROUP):
                        last = nc.tensor.transpose(bank[4 + k][:, j * P:(j + 1) * P],
                                                   x1_group[:, j, k * P:(k + 1) * P], const("ident"))
                    last.then_inc(x1T_psum, 1)

            def group_step(g, has_next):
                pe.wait_ge(x1T_low, 2 * g + 2)
                for f in range(FB):
                    if f >= RING or starts_late(g):
                        pe.wait_ge(h_act, g * FB + f - RING + 1)
                    for k in range(KT):
                        last = split_product(bank[f % RING], [w1_hl[:, i, k, f * P:(f + 1) * P] for i in range(2)],
                                             [x1T_hl[:, i, k, :] for i in range(2)], first=(k == 0), last=(k == KT - 1))
                    last.then_inc(h_psum, 1)
                if has_next:
                    transpose_x1(g + 1)
                for j in range(GROUP):
                    n = g * GROUP + j
                    if j >= 2 or starts_late(g):
                        pe.wait_ge(y2_added, n - 1)
                    for f in range(FB):
                        if j == 0:
                            pe.wait_ge(h_low, g * FB + f + 1)
                        last = split_product(bank[6 + j % 2][:, 0:DIM], [hT_hl[:, i, f, j * P:(j + 1) * P] for i in range(2)],
                                             [w2_hl[:, i, f, :] for i in range(2)], first=(f == 0), last=(f == FB - 1))
                    last.then_inc(y2_psum, 1)

            pe.wait_ge(w1_low, 2)
            pe.wait_ge(w2_low, 2)
            transpose_x1(0)
            group_step(0, True)
            with pe.Fori(1, GROUPS - 1) as g:
                group_step(g, True)
            group_step(GROUPS - 1, False)


def shape_constants():
    import numpy as np
    cols, ncols = const_columns()
    c = np.zeros((P, ncols), np.float32)
    i = np.arange(P)
    c[:, slice(*cols["tri"])] = i[:, None] <= i[None, :]
    c[:, slice(*cols["tri_rest"])] = i[:, None] > i[None, :]
    c[:, slice(*cols["score_mask"])] = (i[:, None] % HALF) <= i[None, :HALF]
    c[:, slice(*cols["head_mask"])] = (i[:, None] // HD) == (i[None, :] // HD)
    c[:, slice(*cols["ident"])] = i[:, None] == i[None, :]
    c[:, cols["even"][0]] = i // HD % 2 == 0
    c[:, cols["odd"][0]] = i // HD % 2 == 1
    half = HD // 2
    exps = np.arange(half, dtype=np.float32) / np.float32(half)
    inv_freq = np.float32(1.0) / np.power(np.float32(10000.0), exps)
    angle = np.arange(SEQ, dtype=np.float32)[:, None] * inv_freq[None, :]
    scale = np.float32(HD ** -0.25)
    cos, sin = np.cos(angle) * scale, np.sin(angle) * scale
    rope = np.concatenate([cos, cos, -sin, sin], axis=1).astype(np.float32)
    sel = np.zeros((2, 4, P), np.float32)
    for fc in range(2):
        for par in range(2):
            sel[fc, 2 * fc + par, par * RANK:(par + 1) * RANK] = 1.0
    return c, rope.reshape(TILES_PER_SEQ, P, 2 * HD), sel


def kernel(L0_attn_x, L0_attn_w_qkv, L0_attn_w_out, L0_ffn_fc1_A, L0_ffn_fc1_B, L0_ffn_fc2_A, L0_ffn_fc2_B,
           L0_ffn_fc1_logits, L0_ffn_fc2_logits):
    import numpy as np
    import concourse.bacc as bacc
    from concourse.bass_utils import run_bass_kernel_spmd

    consts, rope, sel = shape_constants()
    x = np.ascontiguousarray(np.asarray(L0_attn_x)).reshape(TILES * P, DIM)
    xT = x.reshape(TILES, P, KT, P).transpose(0, 3, 2, 1).reshape(TILES, P, DIM)
    xin = np.concatenate([xT, np.tile(rope, (BATCH, 1, 1))], axis=2)
    a1, b1 = np.asarray(L0_ffn_fc1_A), np.asarray(L0_ffn_fc1_B)
    a2, b2 = np.asarray(L0_ffn_fc2_A), np.asarray(L0_ffn_fc2_B)
    arrays = {
        "xin": np.ascontiguousarray(xin),
        "x": x,
        "w_qkv": np.ascontiguousarray(np.asarray(L0_attn_w_qkv)),
        "w_out": np.ascontiguousarray(np.asarray(L0_attn_w_out)),
        "consts": consts,
        "selectors": sel,
        "logits": np.stack([np.asarray(L0_ffn_fc1_logits), np.asarray(L0_ffn_fc2_logits)]),
        "factors1": np.ascontiguousarray(np.concatenate([a1.transpose(0, 2, 1), b1], axis=2)),
        "factors2": np.ascontiguousarray(np.concatenate([b2, a2.transpose(0, 2, 1)], axis=2)),
    }
    nc = bacc.Bacc("TRN2", target_bir_lowering=False, num_devices=1)
    ap = {n: nc.dram_tensor(n, a.shape, mybir.dt.from_np(a.dtype), kind="ExternalInput").ap() for n, a in arrays.items()}
    out = nc.dram_tensor("out", (TILES * P, DIM), F32, kind="ExternalOutput").ap()
    build_program(nc, ap["xin"], ap["x"], ap["w_qkv"], ap["w_out"], ap["consts"], ap["selectors"], ap["logits"],
                  (ap["factors1"], ap["factors2"]), out)
    r = run_bass_kernel_spmd(nc, [arrays], core_ids=[0])
    return r.results[0]["out"].reshape(BATCH, SEQ, DIM)
```

```python
from contextlib import ExitStack

import concourse.bass as bass
from concourse import mybir

F32 = mybir.dt.float32
F32R = mybir.dt.float32r
U32 = mybir.dt.uint32
ALU = mybir.AluOpType
ACT = mybir.ActivationFunctionType
AX = mybir.AxisListType

P = 128
BATCH, SEQ, DIM = 8, 1024, 256
HEADS, HD = 16, 16
HALF = 64
TILES = BATCH * SEQ // P
TILES_PER_SEQ = SEQ // P
KT = DIM // P
FFN = 1024
PRIMS, TOPK, RANK = 64, 32, 64
PAIRS = TOPK // 2
SLOTS = 4
ROUNDS = PAIRS // SLOTS
GROUP = 4
GROUPS = TILES // GROUP
FB = FFN // P
RING = 4
SPLITS = 2
LARGE_HALVES = (slice(DIM, DIM + FFN // 2), slice(DIM + FFN // 2, DIM + FFN))
LN_EPS = 1e-5
DEN_MIN = 1e-6
NEG = -3.0e38
CONSTS = dict(tri=P, tri_rest=P, score_mask=HALF, head_mask=P, ident=P, even=1, odd=1)


def const_columns():
    at, out = 0, {}
    for name, n in CONSTS.items():
        out[name] = (at, at + n)
        at += n
    return out, at


def build_program(nc, xT, x, w_qkv, w_out, consts, rope_table, logits, factors, out):
    with ExitStack() as ctx:
        def sb(name, shape, dt=F32):
            return ctx.enter_context(nc.sbuf_tensor(name, shape, dt))

        def sem(name):
            return ctx.enter_context(nc.semaphore(name))

        psum = ctx.enter_context(nc.psum_tensor("psum", [P, 8, 512], F32))
        bank = [psum[:, i, :] for i in range(8)]

        stream = sb("stream", [P, TILES, DIM])
        cols, ncols = const_columns()
        const_sb = sb("const_sb", [P, ncols])

        def const(name):
            return const_sb[:, cols[name][0]:cols[name][1]]

        wqkv_hl = sb("wqkv_hl", [P, 2, KT, 3 * DIM], F32R)
        wout_hl = sb("wout_hl", [P, 2, KT, DIM], F32R)
        logit_sb = sb("logit_sb", [2, PRIMS])
        top_val = sb("top_val", [2, TOPK])
        top_idx = sb("top_idx", [2, TOPK], U32)
        neg_max = sb("neg_max", [2, 1])
        top_exp = sb("top_exp", [2, TOPK])
        top_sum = sb("top_sum", [2, 1])
        top_inv = sb("top_inv", [2, 1])
        top_w = sb("top_w", [2, 2, TOPK])
        top_scaled = sb("top_scaled", [2, TOPK])
        factor_w = sb("factor_w", [P, 2, PAIRS])
        xT_in = sb("xT_in", [P, 2, DIM])
        rope_tab = sb("rope_tab", [P, TILES_PER_SEQ, 2 * HD])
        scratch = sb("scratch", [P, 5, 2 * DIM])
        rope_cos, rope_sin, roped, feat_exp, feat_relu = (scratch[:, i] for i in range(5))
        feat = sb("feat", [P, 2, 2 * DIM])
        values = sb("values", [P, 2, DIM])
        v_pairs = sb("v_pairs", [P, 2, 2, HEADS // 2, 2 * HD])
        den = sb("den", [P, HEADS])
        den_max = sb("den_max", [P, HEADS])
        den_inv = sb("den_inv", [P, HEADS])
        q_norm = sb("q_norm", [P, DIM])
        den_prod = q_norm
        qT = sb("qT", [P, KT, P])
        qT_heads = sb("qT_heads", [P, KT, 2, P])
        kT = sb("kT", [P, KT, P])
        state_sb = sb("state_sb", [P, 2, 2, KT, P])
        scores_sb = sb("scores_sb", [P, 4, 4, HALF])
        oT = sb("oT", [P, KT, P])
        fence_out = sb("fence_out", [P, 1])
        stats1 = sb("stats1", [P, TILES, 6])
        mean1 = sb("mean1", [P, TILES])
        moment_sum, moment_dif, moment_m2, moment_var, moment_sq = (
            scratch[:, 4, i * TILES:(i + 1) * TILES] for i in range(5))
        var1 = sb("var1", [P, TILES])
        exponent = sb("exponent", [P, TILES])
        rstd1 = sb("rstd1", [P, TILES])
        slot = sb("slot", [P, SLOTS, DIM + FFN])
        raw = slot[:, 2:4].rearrange("p a b -> p (a b)")
        raw_qkv = raw[:, 0:KT * 3 * DIM]
        raw_out = raw[:, KT * 3 * DIM:KT * 4 * DIM]
        split_store = sb("split_store", [P, 2 * FB * GROUP * P], F32R)
        factor_hl = split_store[:, 0:2 * SPLITS * (DIM + FFN)].rearrange("p (a s c) -> p a s c", a=2, s=SPLITS)
        xo = split_store[:, 2 * SPLITS * (DIM + FFN):][:, 0:6 * DIM].rearrange("p (a n) -> p a n", n=DIM)
        xT_high, xT_low = xo[:, 0:2], xo[:, 2:4]
        oT_high, oT_low = (xo[:, i].rearrange("p (k n) -> p k n", k=KT) for i in (4, 5))
        hT_hl = split_store[:].rearrange("p (a f n) -> p a f n", a=2, f=FB)
        w1_hl = sb("w1_hl", [P, 2, KT, FFN], F32R)
        w2_hl = sb("w2_hl", [P, 2, FB, DIM], F32R)
        k_hl = w1_hl[:, 0, 0, :].rearrange("p (t a n) -> p t a n", t=2, a=2)
        tri_r = w1_hl[:, 0, 1, 0:2 * P].rearrange("p (a n) -> p a n", a=2)
        gelu_out = scratch[:, 0:2]
        x1_group = scratch[:, 2:4].rearrange("p a b -> p (a b)").rearrange("p (t d) -> p t d", t=GROUP)
        x1T_hl = wqkv_hl[:].rearrange("p a k n -> p (a k n)")[:, 0:2 * KT * GROUP * P]\
            .rearrange("p (a k n) -> p a k n", a=2, k=KT)
        stats2 = sb("stats2", [P, GROUP, 6])
        mean2 = sb("mean2", [P, GROUP])
        var2 = sb("var2", [P, GROUP])
        rstd2 = sb("rstd2", [P, GROUP])

        b_qk, b_y, b_acc, b_o = bank[0:4]
        b_ksum, b_state = b_acc[:, 0:DIM], b_acc[:, DIM:2 * DIM]
        b_v = b_y[:, DIM:2 * DIM]
        b_scores = psum[:, 4:8, :]
        b_kT, b_qT = bank[6][:, 0:DIM], bank[7][:, 0:DIM]

        def flat(a):
            return a.rearrange("p a d -> p (a d)")

        s_logits, s_const, s_rope, s_wout = (sem(n) for n in (
            "logits_loaded", "const_loaded", "rope_loaded", "wout_loaded"))
        s_wqkv = [sem(f"wqkv_loaded{k}") for k in range(KT)]
        s_xin = [sem("xin_loaded0"), sem("xin_loaded1")]
        s_res = [sem("residual_loaded0"), sem("residual_loaded1")]
        s_slot = [sem(f"slot_loaded{s}") for s in range(SLOTS)]
        (topk_step, topk_done, top_exp_done, top_w_done, bcast_ready, factor_w_ready, zeroed, w_high, w_low) = (
            sem(n) for n in ("topk_step", "topk_done", "top_exp_done", "top_w_done", "bcast_ready",
                             "factor_w_ready", "zeroed", "w_high", "w_low"))
        (qT_summed, k_high, k_low, x_high, x_low, qk_ready, v_ready, qk_used, v_used, v_spread,
         roped_ready, exp_done, relu_done, feat_ready, carry_ready, ksum_ready, ksum_used, den_done,
         den_max_done, den_inv_done, qnorm_ready,
         state_ready, mid_ready, kT_psum, qT_psum, kT_ready, qT_ready, scores_ready,
         scores_masked, o_ready, o_high, o_used, o_low, y_ready, y_used, stats1_ready) = (sem(n) for n in (
             "qT_summed", "k_high", "k_low", "x_high", "x_low", "qk_ready", "v_ready", "qk_used", "v_used",
             "v_spread", "roped_ready", "exp_done", "relu_done", "feat_ready", "carry_ready", "ksum_ready",
             "ksum_used", "den_done", "den_max_done", "den_inv_done",
             "qnorm_ready", "state_ready", "mid_ready", "kT_psum", "qT_psum",
             "kT_ready", "qT_ready", "scores_ready", "scores_masked", "o_ready", "o_high", "o_used", "o_low",
             "y_ready", "y_used", "stats1_ready"))
        (factor_high, factor_low, pair_summed, moment_step, w1_high, w1_low, w2_high, w2_low, var1_ready,
         rstd1_ready) = (sem(n) for n in (
             "factor_high", "factor_low", "pair_summed", "moment_step", "w1_high", "w1_low",
             "w2_high", "w2_low", "var1_ready", "rstd1_ready"))
        (x1_ready, x1_copied, x1T_psum, x1T_high, x1T_low, h_psum, h_act, h_low, y2_psum, y2_added,
         stats2_ready, var2_ready, rstd2_ready, result_ready, stored) = (sem(n) for n in (
             "x1_ready", "x1_copied", "x1T_psum", "x1T_high", "x1T_low", "h_psum", "h_act",
             "h_low", "y2_psum", "y2_added", "stats2_ready", "var2_ready", "rstd2_ready", "result_ready",
             "stored"))

        block = ctx.enter_context(nc.Block())

        def tile_loop(engine, step):
            for t in range(3):
                step(t, t % 2, t // 2 + 1)
            with engine.Fori(2, TILES // 2 - 1) as i:
                step(2 * i - 1, 1, i)
                step(2 * i, 0, i + 1)
            for t in range(TILES - 3, TILES):
                step(t, t % 2, t // 2 + 1)

        def at(t, least):
            return t >= least if isinstance(t, int) else True

        def before(t, end):
            return t < end if isinstance(t, int) else True

        def group_loop(engine, step):
            step(0, True, True)
            with engine.Fori(1, GROUPS - 2) as g:
                step(g, True, True)
            step(GROUPS - 2, True, False)
            step(GROUPS - 1, False, False)

        def starts_late(g):
            return not isinstance(g, int) or g > 0

        @block.sync
        def _(sp):
            tokens = x.rearrange("(t p) d -> t p d", p=P)

            def load_tile(t, p):
                sp.dma_start(xT_in[:, p, :], xT[bass.ds(t, 1)].rearrange("a p c -> (a p) c")).then_inc(s_xin[p], 16)
                sp.dma_start(flat(stream[:, bass.ds(t, 1), :]), tokens[bass.ds(t, 1)].rearrange("a p c -> (a p) c"))\
                    .then_inc(s_res[p], 16)

            sp.dma_start(logit_sb[:], logits).then_inc(s_logits, 16)
            qkv_rows = w_qkv.rearrange("(k p) n -> p k n", p=P)
            for k in range(KT):
                sp.dma_start(raw_qkv[:, k * 3 * DIM:(k + 1) * 3 * DIM], qkv_rows[:, k, :]).then_inc(s_wqkv[k], 16)
                load_tile(k, k)
            sp.dma_start(const_sb[:], consts).then_inc(s_const, 16)
            sp.dma_start(rope_tab[:], rope_table).then_inc(s_rope, 16)
            sp.dma_start(raw_out.rearrange("p (k n) -> p k n", k=KT), w_out.rearrange("(k p) n -> p k n", p=P))\
                .then_inc(s_wout, 16)

            def gather(fc, n, s, first):
                if not first:
                    sp.wait_ge(factor_low, fc * PAIRS + n - SLOTS + 1)
                for half in range(2):
                    k = sp.value_load(top_idx[fc:fc + 1, bass.ds(2 * n + half, 1)], min_val=0, max_val=PRIMS - 1)
                    sp.dma_start(slot[half * RANK:(half + 1) * RANK, s, :],
                                 factors[fc][bass.ds(k, 1)].rearrange("a r c -> (a r) c")).then_inc(s_slot[s], 16)

            def next_tile(t, p):
                sp.wait_ge(x_low, t - 1)
                load_tile(t, p)

            next_tile(2, 0)
            next_tile(3, 1)
            sp.wait_ge(topk_done, 1)
            sp.wait_ge(w_low, KT + 1)
            for s in range(SLOTS):
                gather(0, s, s, True)

            with sp.Fori(2, TILES // 2) as i:
                next_tile(2 * i, 0)
                next_tile(2 * i + 1, 1)
            with sp.Fori(1, ROUNDS) as r:
                for s in range(SLOTS):
                    gather(0, r * SLOTS + s, s, False)
            for s in range(SLOTS):
                gather(1, s, s, False)

            def copy_x1(g):
                sp.wait_ge(x1_ready, (g + 1) * GROUP)
                if starts_late(g):
                    sp.wait_ge(x1T_psum, 2 * g)
                sp.dma_start(x1_group, stream[:, bass.ds(g * GROUP, GROUP), :]).then_inc(x1_copied, 16)

            copy_x1(0)
            with sp.Fori(1, ROUNDS) as r:
                for s in range(SLOTS):
                    gather(1, r * SLOTS + s, s, False)
            result_out = out.rearrange("(g t p) d -> g p t d", t=GROUP, p=P)

            def group_step(g, has_next, has_third):
                if has_third:
                    copy_x1(g + 2)
                sp.wait_ge(result_ready, g + 1)
                sp.dma_start(result_out[bass.ds(g, 1)].rearrange("a p t d -> p (a t) d"),
                             stream[:, bass.ds(g * GROUP, GROUP), :]).then_inc(stored, 16)

            copy_x1(1)
            group_loop(sp, group_step)
            sp.wait_ge(stored, 16 * GROUPS)

        @block.gpsimd
        def _(pool):
            def rope_sum(n):
                pool.wait_ge(qk_used, n + 1)
                if at(n, 1):
                    pool.wait_ge(relu_done, n)
                nc.gpsimd.tensor_tensor(roped, rope_cos, rope_sin, ALU.add).then_inc(roped_ready, 1)

            def split_x(n, p):
                pool.wait_ge(x_high, n + 1)
                nc.gpsimd.tensor_tensor(xT_low[:, p], xT_in[:, p], xT_high[:, p].bitcast(F32),
                                        ALU.subtract).then_inc(x_low, 1)

            def split_k(n, p):
                pool.wait_ge(k_high, n + 1)
                nc.gpsimd.tensor_tensor(k_hl[:, p, 1], feat[:, p, DIM:2 * DIM], k_hl[:, p, 0].bitcast(F32),
                                        ALU.subtract).then_inc(k_low, 1)

            def sum_q(n):
                pool.wait_ge(qT_ready, 2 * n + 2)
                nc.gpsimd.tensor_tensor(qT[:], qT_heads[:, :, 0, :], qT_heads[:, :, 1, :], ALU.add).then_inc(qT_summed, 1)

            def split_o(n):
                pool.wait_ge(o_used, n + 1)
                if at(n, 1):
                    pool.wait_ge(y_ready, n)
                nc.gpsimd.tensor_tensor(oT_low, oT[:], oT_high.bitcast(F32), ALU.subtract).then_inc(o_low, 1)

            def step(t, parity, number):
                if at(t, 1):
                    split_o(t - 1)
                sum_q(t)
                if before(t, TILES - 3):
                    split_x(t + 3, 1 - parity)
                if before(t, TILES - 1):
                    split_k(t + 1, 1 - parity)
                if before(t, TILES - 2):
                    rope_sum(t + 2)

            nc.gpsimd.memset(v_pairs[:], 0.0).then_inc(zeroed, 1)
            nc.gpsimd.memset(exponent[:], -0.5).then_inc(zeroed, 1)
            split_x(0, 0)
            split_x(1, 1)
            rope_sum(0)
            split_x(2, 0)
            split_k(0, 0)
            rope_sum(1)
            tile_loop(pool, step)
            split_o(TILES - 1)
            pool.wait_ge(var1_ready, 1)
            pool.wait_ge(zeroed, 2)
            nc.gpsimd.tensor_tensor(rstd1[:], var1[:], exponent[:], ALU.pow).then_inc(rstd1_ready, 1)
            with pool.Fori(0, GROUPS) as g:
                pool.wait_ge(var2_ready, g + 1)
                nc.gpsimd.tensor_tensor(rstd2[:], var2[:], exponent[:, 0:GROUP], ALU.pow).then_inc(rstd2_ready, 1)

        @block.scalar
        def _(act):
            copy = nc.scalar.activation

            def split_x(n, p, loads):
                act.wait_ge(s_xin[p], 16 * loads)
                if not (isinstance(n, int) and n < 2):
                    act.wait_ge(v_ready, n - 1)
                copy(xT_high[:, p], xT_in[:, p], ACT.Copy).then_inc(x_high, 1)

            def move_v(n, p):
                act.wait_ge(v_ready, n + 1)
                copy(values[:, p, :], b_v, ACT.Copy).then_inc(v_used, 1)

            def spread_v(n, p):
                act.wait_ge(v_used, n + 1)
                for odd in range(2):
                    for half in range(2):
                        to = v_pairs[odd * HALF:(odd + 1) * HALF, p, half, :, odd * HD:(odd + 1) * HD]
                        src = values[half * HALF:(half + 1) * HALF, p, :].rearrange("k (a b c) -> k a b c", b=2, c=HD)
                        last = copy(to, src[:, :, odd, :], ACT.Copy)
                last.then_inc(v_spread, 1)

            def split_k(n, p):
                act.wait_ge(feat_ready, n + 1)
                if at(n, 2):
                    act.wait_ge(state_ready, 2 * n - 2)
                copy(k_hl[:, p, 0], feat[:, p, DIM:2 * DIM], ACT.Copy).then_inc(k_high, 1)

            def features(n):
                act.wait_ge(roped_ready, n + 1)
                if at(n, 1):
                    act.wait_ge(feat_ready, n)
                copy(feat_exp, roped, ACT.Exp).then_inc(exp_done, 1)
                copy(feat_relu, roped, ACT.Relu).then_inc(relu_done, 1)

            def move_o(n):
                act.wait_ge(o_ready, n + 1)
                if at(n, 1):
                    act.wait_ge(y_ready, n)
                o = b_o[:, 0:DIM].rearrange("p (k n) -> p k n", k=KT)
                copy(oT_high, o, ACT.Copy).then_inc(o_high, 1)
                copy(oT[:], o, ACT.Copy).then_inc(o_used, 1)

            def step(t, parity, number):
                act.wait_ge(kT_psum, t + 1)
                copy(kT[:], b_kT.rearrange("p (k n) -> p k n", k=KT), ACT.Copy).then_inc(kT_ready, 1)
                if at(t, 1):
                    move_o(t - 1)
                if before(t, TILES - 1):
                    move_v(t + 1, 1 - parity)
                act.wait_ge(qT_psum, t + 1)
                q = b_qT.rearrange("p (k n) -> p k n", k=KT)
                copy(qT_heads[:, :, 0, :], q, ACT.Copy, scale=const("even")).then_inc(qT_ready, 1)
                copy(qT_heads[:, :, 1, :], q, ACT.Copy, scale=const("odd")).then_inc(qT_ready, 1)
                if before(t, TILES - 1):
                    features(t + 1)
                    spread_v(t + 1, 1 - parity)
                if before(t, TILES - 3):
                    split_x(t + 3, 1 - parity, number + 2 if parity == 1 else number + 1)
                if before(t, TILES - 1):
                    split_k(t + 1, 1 - parity)

            split_x(0, 0, 1)
            for k in range(KT):
                act.wait_ge(s_wqkv[k], 16)
                copy(wqkv_hl[:, 0, k, :], raw_qkv[:, k * 3 * DIM:(k + 1) * 3 * DIM], ACT.Copy).then_inc(w_high, 1)
            split_x(1, 1, 1)
            act.wait_ge(s_wout, 16)
            copy(wout_hl[:, 0].rearrange("p k n -> p (k n)"), raw_out, ACT.Copy).then_inc(w_high, 1)
            act.wait_ge(s_const, 16)
            act.wait_ge(topk_done, 1)
            nc.scalar.activation(top_exp[:], top_val[:], ACT.Exp, bias=neg_max[:, 0:1],
                                 accum_out=top_sum[:]).then_inc(top_exp_done, 1)
            copy(tri_r, const_sb[:, 0:2 * P].rearrange("p (a n) -> p a n", a=2), ACT.Copy)
            move_v(0, 0)
            act.wait_ge(zeroed, 2)
            spread_v(0, 0)
            features(0)
            split_x(2, 0, 2)
            split_k(0, 0)
            tile_loop(act, step)

            def move_x1T(g, first_bank):
                for k in range(KT):
                    act.wait_ge(x1T_psum, 2 * g + k + 1)
                    copy(x1T_hl[:, 0, k, :], bank[first_bank + k], ACT.Copy).then_inc(x1T_high, 1)

            def split_factors(fc, n, s):
                act.wait_ge(s_slot[s], 32 * (fc * ROUNDS + n + 1))
                pair = fc * PAIRS + n * SLOTS + s
                if not (isinstance(n, int) and fc == 0 and n == 0 and s < SPLITS):
                    act.wait_ge(pair_summed, pair - SPLITS + 1)
                copy(factor_hl[:, 0, s % SPLITS, 0:DIM], slot[:, s, 0:DIM], ACT.Copy,
                     scale=factor_w[:, fc, bass.ds(n * SLOTS + s, 1)]).then_inc(factor_high, 1)
                for part in LARGE_HALVES:
                    copy(factor_hl[:, 0, s % SPLITS, part], slot[:, s, part], ACT.Copy).then_inc(factor_high, 1)

            act.wait_ge(factor_w_ready, 1)
            for s in range(SLOTS):
                split_factors(0, 0, s)
                if s == SPLITS - 1:
                    move_o(TILES - 1)
            with act.Fori(1, ROUNDS) as n:
                for s in range(SLOTS):
                    split_factors(0, n, s)
            for s in range(SLOTS):
                split_factors(1, 0, s)
                if s == 0:
                    act.wait_ge(pair_summed, PAIRS)
                copy(w1_hl[:, 0, s // 2, s % 2 * 512:(s % 2 + 1) * 512], bank[s], ACT.Copy).then_inc(w1_high, 1)
            with act.Fori(1, ROUNDS - 1) as n:
                for s in range(SLOTS):
                    split_factors(1, n, s)
            for s in range(SLOTS):
                split_factors(1, ROUNDS - 1, s)
                if s == 0:
                    move_x1T(0, 0)
            act.wait_ge(pair_summed, 2 * PAIRS)
            for k in range(2):
                copy(w2_hl[:, 0, 4 * k:4 * k + 4, :].rearrange("p (c f) n -> p c (f n)", c=2),
                     psum[:, 4 + 2 * k:6 + 2 * k, :], ACT.Copy).then_inc(w2_high, 1)

            def group_step(g, has_next, has_third):
                for f in range(FB):
                    act.wait_ge(h_psum, g * FB + f + 1)
                    if f == 0 and starts_late(g):
                        act.wait_ge(y2_psum, g * GROUP)
                    copy(hT_hl[:, 0, f, :], bank[f % RING], ACT.Gelu_apprx_tanh)
                    if f >= 2 or starts_late(g):
                        act.wait_ge(h_low, g * FB + f - 1)
                    copy(gelu_out[:, f % 2], bank[f % RING], ACT.Gelu_apprx_tanh).then_inc(h_act, 1)
                if has_next:
                    move_x1T(g + 1, 4)

            group_loop(act, group_step)

        @block.vector
        def _(dve):
            steps = [0]

            def chained(instruction):
                steps[0] += 1
                instruction.then_inc(topk_step, 1)
                dve.wait_ge(topk_step, steps[0])

            dve.wait_ge(s_logits, 16)
            for r in range(TOPK // 8):
                eight = slice(8 * r, 8 * r + 8)
                chained(nc.vector.max(top_val[:, eight], logit_sb[:]))
                chained(nc.vector.max_index(top_idx[:, eight], top_val[:, eight], logit_sb[:]))
                if r < TOPK // 8 - 1:
                    chained(nc.vector.match_replace(logit_sb[:], top_val[:, eight], logit_sb[:], NEG))
            nc.vector.tensor_scalar(neg_max[:], top_val[:, 0:1], -1.0, None, ALU.mult).then_inc(topk_done, 1)
            for k in range(KT):
                dve.wait_ge(w_high, k + 1)
                nc.vector.tensor_tensor(wqkv_hl[:, 1, k, :], raw_qkv[:, k * 3 * DIM:(k + 1) * 3 * DIM],
                                        wqkv_hl[:, 0, k, :].bitcast(F32), ALU.subtract).then_inc(w_low, 1)
            dve.wait_ge(s_rope, 16)
            dve.wait_ge(s_const, 16)

            def rope(n):
                dve.wait_ge(qk_ready, n + 1)
                if at(n, 1):
                    dve.wait_ge(roped_ready, n)
                qk = b_qk.rearrange("p (h c) -> p h c", c=HD)
                position = n % TILES_PER_SEQ
                cos = rope_tab[:, bass.ds(position, 1), 0:HD].broadcast_to([P, 2 * HEADS, HD])
                nc.vector.tensor_tensor(rope_cos.rearrange("p (h c) -> p h c", c=HD), qk, cos, ALU.mult)
                half = HD // 2
                for a, b in ((0, half), (half, 0)):
                    sin = rope_tab[:, bass.ds(position, 1), HD + a:HD + a + half].broadcast_to([P, 2 * HEADS, half])
                    last = nc.vector.tensor_tensor(rope_sin.rearrange("p (h c) -> p h c", c=HD)[:, :, a:a + half],
                                                   qk[:, :, b:b + half], sin, ALU.mult)
                last.then_inc(qk_used, 1)

            def finish_features(n, p):
                dve.wait_ge(exp_done, n + 1)
                dve.wait_ge(relu_done, n + 1)
                nc.vector.scalar_tensor_tensor(out=feat[:, p, :], in0=feat_exp, scalar=1.0, in1=feat_relu,
                                               op0=ALU.min, op1=ALU.add).then_inc(feat_ready, 1)

            def mask_state(p, which):
                return nc.vector.tensor_tensor(
                    state_sb[:, p, which], b_state.rearrange("p (k n) -> p k n", k=KT),
                    const("head_mask").unsqueeze(1).broadcast_to([P, KT, P]), ALU.mult)

            def carry(t, p, new_sequence):
                if new_sequence is True:
                    nc.vector.memset(b_acc, 0.0).then_inc(topk_step, 1)
                    dve.wait_ge(topk_step, steps[0] + 1)
                elif new_sequence is not None:
                    with dve.If_eq(dve.to_reg(new_sequence % (TILES_PER_SEQ // 2)), 0):
                        dve.wait_ge(state_ready, 2 * t)
                        nc.vector.memset(b_acc, 0.0)
                        nc.vector.drain()
                if at(t, 1):
                    dve.wait_ge(state_ready, 2 * t)
                mask_state(p, 0).then_inc(carry_ready, 1)

            def fence(semaphore, value):
                dve.wait_ge(semaphore, value)
                nc.vector.tensor_copy(fence_out[:], const("even"))

            def moments(stats, n, base, mean, var, signal):
                v = nc.vector
                v.tensor_tensor(moment_sum[:, 0:n], stats[:, :, 1], stats[:, :, 4], ALU.add)
                v.tensor_tensor(moment_dif[:, 0:n], stats[:, :, 1], stats[:, :, 4], ALU.subtract)
                v.tensor_tensor(moment_m2[:, 0:n], stats[:, :, 2], stats[:, :, 5], ALU.add).then_inc(moment_step, 1)
                dve.wait_ge(moment_step, base + 1)
                v.tensor_scalar(mean[:], moment_sum[:, 0:n], 0.5, None, ALU.mult)
                v.tensor_tensor(moment_sq[:, 0:n], moment_dif[:, 0:n], moment_dif[:, 0:n], ALU.mult)
                v.tensor_scalar(moment_var[:, 0:n], moment_m2[:, 0:n], 1.0 / DIM, LN_EPS, ALU.mult, ALU.add)\
                    .then_inc(moment_step, 1)
                dve.wait_ge(moment_step, base + 2)
                v.scalar_tensor_tensor(out=var[:], in0=moment_sq[:, 0:n], scalar=0.25, in1=moment_var[:, 0:n],
                                       op0=ALU.mult, op1=ALU.add).then_inc(signal, 1)

            def layer_norm1(n, p, loads):
                dve.wait_ge(s_res[p], 16 * loads)
                dve.wait_ge(y_ready, n + 1)
                if before(n, TILES - 3):
                    dve.wait_ge(v_used, n + 4)
                row = flat(stream[:, bass.ds(n, 1), :])
                nc.vector.tensor_tensor(row, b_y[:, 0:DIM], row, ALU.add).then_inc(y_used, 1)
                fence(y_used, n + 1)
                nc.vector.bn_stats(flat(stats1[:, bass.ds(n, 1), :]), row).then_inc(stats1_ready, 1)

            def step(t, parity, number):
                dve.wait_ge(ksum_ready, t + 1)
                nc.vector.tensor_tensor(den_prod[:], feat[:, parity, 0:DIM], b_ksum, ALU.mult).then_inc(ksum_used, 1)
                dve.wait_ge(ksum_used, t + 1)
                nc.vector.tensor_reduce(den[:], den_prod[:].rearrange("p (h c) -> p h c", c=HD), AX.X, ALU.add)\
                    .then_inc(den_done, 1)
                dve.wait_ge(den_done, t + 1)
                nc.vector.tensor_scalar(den_max[:], den[:], DEN_MIN, None, ALU.max).then_inc(den_max_done, 1)
                dve.wait_ge(den_max_done, t + 1)
                nc.vector.reciprocal(den_inv[:], den_max[:]).then_inc(den_inv_done, 1)
                dve.wait_ge(den_inv_done, t + 1)
                nc.vector.tensor_tensor(q_norm[:].rearrange("p (h c) -> p h c", c=HD),
                                        feat[:, parity, 0:DIM].rearrange("p (h c) -> p h c", c=HD),
                                        den_inv[:].unsqueeze(2).broadcast_to([P, HEADS, HD]), ALU.mult).then_inc(qnorm_ready, 1)
                dve.wait_ge(state_ready, 2 * t + 1)
                mask_state(parity, 1).then_inc(mid_ready, 1)
                if at(t, 2):
                    layer_norm1(t - 2, parity, number - 1)
                for part in range(2):
                    dve.wait_ge(scores_ready, 2 * t + part + 1)
                    tiles = slice(2 * part, 2 * part + 2)
                    nc.vector.tensor_tensor(
                        scores_sb[:, tiles], b_scores[:, tiles, 0:4 * HALF].rearrange("p r (h q) -> p r h q", h=4),
                        const("score_mask").unsqueeze(1).unsqueeze(1).broadcast_to([P, 2, 4, HALF]),
                        ALU.mult).then_inc(scores_masked, 1)
                    if part == 0 and before(t, TILES - 1):
                        finish_features(t + 1, 1 - parity)
                    if part == 0 and before(t, TILES - 2):
                        rope(t + 2)
                if before(t, TILES - 1):
                    carry(t + 1, 1 - parity, number if parity == 1 and not isinstance(t, int) else None)

            rope(0)
            dve.wait_ge(w_high, KT + 1)
            nc.vector.tensor_tensor(wout_hl[:, 1].rearrange("p k n -> p (k n)"), raw_out,
                                    wout_hl[:, 0].rearrange("p k n -> p (k n)").bitcast(F32), ALU.subtract).then_inc(w_low, 1)
            dve.wait_ge(top_exp_done, 1)
            chained(nc.vector.reciprocal(top_inv[:], top_sum[:]))
            chained(nc.vector.tensor_scalar(top_scaled[:], top_exp[:], top_inv[:, 0:1], None, ALU.mult))
            for fc in range(2):
                last = nc.vector.tensor_scalar(top_w[:, fc, :], top_scaled[:], const("ident")[0:2, fc:fc + 1], None, ALU.mult)
            last.then_inc(top_w_done, 1)
            finish_features(0, 0)
            dve.wait_ge(bcast_ready, 1)
            nc.vector.tensor_copy(factor_w[:], b_o[:, 0:2 * PAIRS].rearrange("p (f n) -> p f n", f=2))\
                .then_inc(factor_w_ready, 1)
            carry(0, 0, True)
            rope(1)
            tile_loop(dve, step)

            def split_factors(fc, n, s):
                pair = fc * PAIRS + n * SLOTS + s
                high, low = factor_hl[:, 0, s % SPLITS], factor_hl[:, 1, s % SPLITS]
                dve.wait_ge(s_slot[s], 32 * (fc * ROUNDS + n + 1))
                dve.wait_ge(factor_high, 3 * pair + 1)
                nc.vector.scalar_tensor_tensor(out=low[:, 0:DIM], in0=slot[:, s, 0:DIM],
                                               scalar=factor_w[:, fc, bass.ds(n * SLOTS + s, 1)],
                                               in1=high[:, 0:DIM].bitcast(F32), op0=ALU.mult, op1=ALU.subtract)
                for i, part in enumerate(LARGE_HALVES):
                    dve.wait_ge(factor_high, 3 * pair + 2 + i)
                    last = nc.vector.tensor_tensor(low[:, part], slot[:, s, part], high[:, part].bitcast(F32), ALU.subtract)
                last.then_inc(factor_low, 1)

            def normalise1(g):
                for j in range(GROUP):
                    t = g * GROUP + j
                    row = flat(stream[:, bass.ds(t, 1), :])
                    nc.vector.tensor_scalar(row, row, mean1[:, bass.ds(t, 1)],
                                            rstd1[:, bass.ds(t, 1)], ALU.subtract, ALU.mult).then_inc(x1_ready, 1)

            def split_x1T(g, first_bank):
                for k in range(KT):
                    dve.wait_ge(x1T_high, 2 * g + k + 1)
                    nc.vector.tensor_tensor(x1T_hl[:, 1, k, :], bank[first_bank + k], x1T_hl[:, 0, k, :].bitcast(F32),
                                            ALU.subtract).then_inc(x1T_low, 1)

            for s in range(SLOTS):
                split_factors(0, 0, s)
                if s == SPLITS - 1:
                    for n in (TILES - 2, TILES - 1):
                        layer_norm1(n, n % 2, TILES // 2)
                    dve.wait_ge(stats1_ready, TILES)
                    moments(stats1, TILES, 0, mean1, var1, var1_ready)
            with dve.Fori(1, ROUNDS) as n:
                for s in range(SLOTS):
                    split_factors(0, n, s)
            for s in range(SLOTS):
                split_factors(1, 0, s)
                dve.wait_ge(w1_high, s + 1)
                part = slice(s % 2 * 512, (s % 2 + 1) * 512)
                nc.vector.tensor_tensor(w1_hl[:, 1, s // 2, part], bank[s], w1_hl[:, 0, s // 2, part].bitcast(F32),
                                        ALU.subtract).then_inc(w1_low, 1)
                if s == 0:
                    dve.wait_ge(rstd1_ready, 1)
                    normalise1(0)
            with dve.Fori(1, ROUNDS - 1) as n:
                for s in range(SLOTS):
                    split_factors(1, n, s)
            for s in range(SLOTS):
                split_factors(1, ROUNDS - 1, s)
                if s == 0:
                    split_x1T(0, 0)
            for k in range(2):
                dve.wait_ge(w2_high, k + 1)
                high, low = (w2_hl[:, i, 4 * k:4 * k + 4, :].rearrange("p (c f) n -> p c (f n)", c=2) for i in range(2))
                nc.vector.tensor_tensor(low, psum[:, 4 + 2 * k:6 + 2 * k, :], high.bitcast(F32),
                                        ALU.subtract).then_inc(w2_low, 1)

            def finish_group(g):
                dve.wait_ge(rstd2_ready, g + 1)
                for j in range(GROUP):
                    row = flat(stream[:, bass.ds(g * GROUP + j, 1), :])
                    last = nc.vector.tensor_scalar(row, row, mean2[:, j:j + 1], rstd2[:, j:j + 1], ALU.subtract, ALU.mult)
                last.then_inc(result_ready, 1)

            def group_step(g, has_next, has_third):
                for f in range(FB):
                    if f == 2 and starts_late(g):
                        finish_group(g - 1)
                    dve.wait_ge(h_act, g * FB + f + 1)
                    nc.vector.tensor_tensor(hT_hl[:, 1, f, :], gelu_out[:, f % 2], hT_hl[:, 0, f, :].bitcast(F32),
                                            ALU.subtract).then_inc(h_low, 1)
                if has_next:
                    split_x1T(g + 1, 4)
                for j in range(GROUP):
                    n = g * GROUP + j
                    row = flat(stream[:, bass.ds(n, 1), :])
                    dve.wait_ge(y2_psum, n + 1)
                    dve.wait_ge(x1_ready, n + 1)
                    nc.vector.tensor_tensor(row, bank[6 + j % 2][:, 0:DIM], row, ALU.add).then_inc(y2_added, 1)
                    fence(y2_added, n + 1)
                    nc.vector.bn_stats(stats2[:, j, :], row).then_inc(stats2_ready, 1)
                    if j == 0 and has_third:
                        normalise1(g + 2)
                dve.wait_ge(stats2_ready, (g + 1) * GROUP)
                moments(stats2, GROUP, 2 + 2 * g, mean2, var2, var2_ready)

            normalise1(1)
            group_loop(dve, group_step)
            finish_group(GROUPS - 1)

        @block.tensor
        def _(pe):
            mm = nc.tensor.matmul

            def split_product(to, left, right, start=True, first=True, last=True):
                terms = ((0, 0), (0, 1), (1, 0))
                for i, (a, b) in enumerate(terms):
                    product = mm(to, left[a], right[b], start=start and first and i == 0,
                                 stop=(last and i == 2) or not start, skip_group_check=not start)
                return product

            def project_qk(n, p, products=range(3 * KT)):
                if 0 in products:
                    pe.wait_ge(x_high, n + 1)
                    pe.wait_ge(x_low, n + 1)
                    if at(n, 1):
                        pe.wait_ge(qk_used, n)
                for i in products:
                    k = i // 3
                    x_part, w_part = ((0, 0), (0, 1), (1, 0))[i % 3]
                    last = mm(b_qk, (xT_high, xT_low)[x_part][:, p, k * P:(k + 1) * P], wqkv_hl[:, w_part, k, 0:2 * DIM],
                              start=(i == 0), stop=(i == 3 * KT - 1))
                if 3 * KT - 1 in products:
                    last.then_inc(qk_ready, 1)

            def project_v(n, p):
                if at(n, 1):
                    pe.wait_ge(v_used, n)
                for k in range(KT):
                    last = split_product(b_v, (xT_high[:, p, k * P:(k + 1) * P], xT_low[:, p, k * P:(k + 1) * P]),
                                         (wqkv_hl[:, 0, k, 2 * DIM:], wqkv_hl[:, 1, k, 2 * DIM:]),
                                         first=(k == 0), last=(k == KT - 1))
                last.then_inc(v_ready, 1)

            def output_projection(t):
                pe.wait_ge(o_high, t + 1)
                pe.wait_ge(o_low, t + 1)
                if at(t, 1):
                    pe.wait_ge(y_used, t)
                for k in range(KT):
                    last = split_product(b_y[:, 0:DIM], (oT_high[:, k, :], oT_low[:, k, :]),
                                         (wout_hl[:, 0, k, :], wout_hl[:, 1, k, :]), first=(k == 0), last=(k == KT - 1))
                last.then_inc(y_ready, 1)

            def add_to_state(half, parity):
                rows = slice(half * HALF, (half + 1) * HALF)
                for k in range(KT):
                    block = slice(k * P, (k + 1) * P)
                    last = mm(b_state[:, block], feat[rows, parity, DIM + k * P:DIM + (k + 1) * P],
                              values[rows, parity, block], start=False, stop=True, skip_group_check=True)
                last.then_inc(state_ready, 1)

            def transpose(to, src):
                for k in range(KT):
                    last = nc.tensor.transpose(to[:, k * P:(k + 1) * P], src[:, k * P:(k + 1) * P], const("ident"))
                return last

            def add_keys(which, p):
                for i in range(2):
                    last = mm(b_ksum, tri_r[:, which], k_hl[:, p, i], start=False, stop=True, skip_group_check=True)
                return last

            def running_sum(n, p):
                pe.wait_ge(k_low, n + 1)
                pe.wait_ge(carry_ready, n + 1)
                add_keys(0, p).then_inc(ksum_ready, 1)

            def transpose_k(n, p):
                pe.wait_ge(feat_ready, n + 1)
                transpose(b_kT, feat[:, p, DIM:2 * DIM]).then_inc(kT_psum, 1)

            def scores(part, t):
                for k in range(KT):
                    for half in range(2):
                        span = slice(half * HALF, (half + 1) * HALF)
                        for odd in range(2):
                            if part + k + half == 0 and odd == 1:
                                pe.wait_ge(qT_ready, 2 * t + 2)
                            for r in (2 * part, 2 * part + 1):
                                rows = slice(32 * r, 32 * r + 32)
                                column = (2 * k + half) * HALF
                                last = mm(b_scores[odd * HALF:(odd + 1) * HALF, r, column:column + HALF],
                                          kT[rows, k, span], qT_heads[rows, k, odd, span], start=True, stop=True)
                last.then_inc(scores_ready, 1)

            def step(t, parity, number):
                if before(t, TILES - 1):
                    project_v(t + 1, 1 - parity)
                pe.wait_ge(ksum_used, t + 1)
                pe.wait_ge(v_used, t + 1)
                add_to_state(0, parity)
                pe.wait_ge(qnorm_ready, t + 1)
                transpose(b_qT, q_norm).then_inc(qT_psum, 1)
                if before(t, TILES - 2):
                    project_qk(t + 2, parity, range(0, 4))
                pe.wait_ge(kT_ready, t + 1)
                pe.wait_ge(qT_ready, 2 * t + 1)
                scores(0, t)
                if before(t, TILES - 2):
                    project_qk(t + 2, parity, range(4, 6))
                if at(t, 1):
                    if before(t, TILES - 1):
                        pe.wait_ge(v_used, t + 2)
                    output_projection(t - 1)
                scores(1, t)
                pe.wait_ge(mid_ready, t + 1)
                add_keys(1, parity)
                add_to_state(1, parity)
                pe.wait_ge(qT_summed, t + 1)
                pe.wait_ge(v_spread, t + 1)
                if at(t, 1):
                    pe.wait_ge(o_used, t)
                for k in range(KT):
                    for half in range(2):
                        if half == 1:
                            pe.wait_ge(scores_masked, 2 * t + k + 1)
                        mm(b_o[:, k * P + half * HALF:k * P + (half + 1) * HALF], state_sb[:, parity, half, k, :],
                           qT[:, k, half * HALF:(half + 1) * HALF], start=(half == 0 and k == 0), stop=False,
                           skip_group_check=True)
                if before(t, TILES - 1):
                    running_sum(t + 1, 1 - parity)
                    transpose_k(t + 1, 1 - parity)
                for half in range(2):
                    for k in range(KT):
                        for r in range(4):
                            column = k * P + half * HALF
                            last = mm(b_o[32 * r:32 * r + 32, column:column + HALF], v_pairs[:, parity, half, 4 * k + r, :],
                                      scores_sb[:, r, 2 * k + half, :], start=False, stop=True, skip_group_check=True)
                last.then_inc(o_ready, 1)

            pe.wait_ge(w_high, KT)
            pe.wait_ge(w_low, KT)
            project_qk(0, 0)
            project_v(0, 0)
            pe.wait_ge(s_const, 16)
            pe.wait_ge(top_w_done, 1)
            for fc in range(2):
                for half in range(2):
                    last = mm(b_o[half * RANK:(half + 1) * RANK, fc * PAIRS:(fc + 1) * PAIRS],
                              const("tri")[0:2, RANK:2 * RANK], top_w[:, fc, half:TOPK:2], start=True, stop=True)
            last.then_inc(bcast_ready, 1)
            project_qk(1, 1)
            pe.wait_ge(factor_w_ready, 1)
            pe.wait_ge(w_low, KT + 1)
            transpose_k(0, 0)
            running_sum(0, 0)
            tile_loop(pe, step)
            output_projection(TILES - 1)

            def add_pair(fc, n, s, first):
                pe.wait_ge(factor_low, fc * PAIRS + n * SLOTS + s + 1)
                part = [factor_hl[:, i, s % SPLITS] for i in range(2)]
                if fc == 0:
                    products = [(bank[2 * m + c], slice(m * P, (m + 1) * P), slice(DIM + c * 512, DIM + (c + 1) * 512),
                                 first) for m in range(KT) for c in range(2)]
                else:
                    products = [(bank[4 + f // 2][:, (f % 2) * DIM:(f % 2 + 1) * DIM],
                                 slice(DIM + f * P, DIM + (f + 1) * P), slice(0, DIM), first and f % 2 == 0)
                                for f in range(FB)]
                for to, left, right, start in products:
                    for i, (a, b) in enumerate(((0, 0), (0, 1), (1, 0))):
                        last = mm(to, part[a][:, left], part[b][:, right], start=start and i == 0, stop=True,
                                  skip_group_check=True)
                last.then_inc(pair_summed, 1)

            def transpose_x1(g, first_bank):
                pe.wait_ge(x1_copied, 16 * (g + 1))
                for k in range(KT):
                    for j in range(GROUP):
                        last = nc.tensor.transpose(bank[first_bank + k][:, j * P:(j + 1) * P],
                                                   x1_group[:, j, k * P:(k + 1) * P], const("ident"))
                    last.then_inc(x1T_psum, 1)

            pe.wait_ge(qk_used, TILES)
            pe.wait_ge(o_used, TILES)
            for s in range(SLOTS):
                if s == 0:
                    pe.wait_ge(y_used, TILES)
                add_pair(0, 0, s, s == 0)
            with pe.Fori(1, ROUNDS) as n:
                for s in range(SLOTS):
                    add_pair(0, n, s, False)
            for s in range(SLOTS):
                add_pair(1, 0, s, s == 0)
            pe.wait_ge(w1_low, SLOTS)
            with pe.Fori(1, ROUNDS - 1) as n:
                for s in range(SLOTS):
                    add_pair(1, n, s, False)
            transpose_x1(0, 0)
            for s in range(SLOTS):
                add_pair(1, ROUNDS - 1, s, False)

            def group_step(g, has_next, has_third):
                pe.wait_ge(x1T_low, 2 * g + 2)
                for f in range(FB):
                    if f >= RING or starts_late(g):
                        pe.wait_ge(h_act, g * FB + f - RING + 1)
                    for k in range(KT):
                        last = split_product(bank[f % RING], [w1_hl[:, i, k, f * P:(f + 1) * P] for i in range(2)],
                                             [x1T_hl[:, i, k, :] for i in range(2)], first=(k == 0), last=(k == KT - 1))
                    last.then_inc(h_psum, 1)
                if not starts_late(g):
                    pe.wait_ge(w2_low, 2)
                if has_next:
                    transpose_x1(g + 1, 4)
                for j in range(GROUP):
                    n = g * GROUP + j
                    if j >= 2 or starts_late(g):
                        pe.wait_ge(y2_added, n - 1)
                    for f in range(FB):
                        if j == 0:
                            pe.wait_ge(h_low, g * FB + f + 1)
                        last = split_product(bank[6 + j % 2][:, 0:DIM], [hT_hl[:, i, f, j * P:(j + 1) * P] for i in range(2)],
                                             [w2_hl[:, i, f, :] for i in range(2)], first=(f == 0), last=(f == FB - 1))
                    last.then_inc(y2_psum, 1)

            group_loop(pe, group_step)


def shape_constants():
    import numpy as np
    cols, ncols = const_columns()
    c = np.zeros((P, ncols), np.float32)
    i = np.arange(P)
    c[:, slice(*cols["tri"])] = i[:, None] <= i[None, :]
    c[:, slice(*cols["tri_rest"])] = i[:, None] > i[None, :]
    c[:, slice(*cols["score_mask"])] = (i[:, None] % HALF) <= i[None, :HALF]
    c[:, slice(*cols["head_mask"])] = (i[:, None] // HD) == (i[None, :] // HD)
    c[:, slice(*cols["ident"])] = i[:, None] == i[None, :]
    c[:, cols["even"][0]] = i // HD % 2 == 0
    c[:, cols["odd"][0]] = i // HD % 2 == 1
    half = HD // 2
    exps = np.arange(half, dtype=np.float32) / np.float32(half)
    inv_freq = np.float32(1.0) / np.power(np.float32(10000.0), exps)
    angle = np.arange(SEQ, dtype=np.float32)[:, None] * inv_freq[None, :]
    scale = np.float32(HD ** -0.25)
    cos, sin = np.cos(angle) * scale, np.sin(angle) * scale
    rope = np.concatenate([cos, cos, -sin, sin], axis=1).astype(np.float32)
    return c, np.ascontiguousarray(rope.reshape(TILES_PER_SEQ, P, 2 * HD).transpose(1, 0, 2))


def kernel(L0_attn_x, L0_attn_w_qkv, L0_attn_w_out, L0_ffn_fc1_A, L0_ffn_fc1_B, L0_ffn_fc2_A, L0_ffn_fc2_B,
           L0_ffn_fc1_logits, L0_ffn_fc2_logits):
    import numpy as np
    import concourse.bacc as bacc
    from concourse.bass_utils import run_bass_kernel_spmd

    consts, rope = shape_constants()
    x = np.ascontiguousarray(np.asarray(L0_attn_x)).reshape(TILES * P, DIM)
    xT = np.ascontiguousarray(x.reshape(TILES, P, KT, P).transpose(0, 3, 2, 1)).reshape(TILES, P, DIM)
    a1, b1 = np.asarray(L0_ffn_fc1_A), np.asarray(L0_ffn_fc1_B)
    a2, b2 = np.asarray(L0_ffn_fc2_A), np.asarray(L0_ffn_fc2_B)
    arrays = {
        "xT": xT,
        "x": x,
        "w_qkv": np.ascontiguousarray(np.asarray(L0_attn_w_qkv)),
        "w_out": np.ascontiguousarray(np.asarray(L0_attn_w_out)),
        "consts": consts,
        "rope_table": rope,
        "logits": np.stack([np.asarray(L0_ffn_fc1_logits), np.asarray(L0_ffn_fc2_logits)]),
        "factors1": np.ascontiguousarray(np.concatenate([a1.transpose(0, 2, 1), b1], axis=2)),
        "factors2": np.ascontiguousarray(np.concatenate([b2, a2.transpose(0, 2, 1)], axis=2)),
    }
    nc = bacc.Bacc("TRN2", target_bir_lowering=False, num_devices=1)
    ap = {n: nc.dram_tensor(n, a.shape, mybir.dt.from_np(a.dtype), kind="ExternalInput").ap() for n, a in arrays.items()}
    out = nc.dram_tensor("out", (TILES * P, DIM), F32, kind="ExternalOutput").ap()
    build_program(nc, ap["xT"], ap["x"], ap["w_qkv"], ap["w_out"], ap["consts"], ap["rope_table"], ap["logits"],
                  (ap["factors1"], ap["factors2"]), out)
    r = run_bass_kernel_spmd(nc, [arrays], core_ids=[0])
    return r.results[0]["out"].reshape(BATCH, SEQ, DIM)
```
